# Optimizing a Trainium2 kernel written in Bass

```python
import numpy as np
import jax
import jax.numpy as jnp

def _softmax(x, axis=-1):
    return jax.nn.softmax(x, axis=axis)

def _gelu(x):
    return jax.nn.gelu(x, approximate=True)

def _silu(x):
    return jax.nn.silu(x)

def _sigmoid(x):
    return jax.nn.sigmoid(x)

def _layernorm(x, axis=-1, eps=1e-05):
    m = jnp.mean(x, axis=axis, keepdims=True)
    v = jnp.var(x, axis=axis, keepdims=True)
    return (x - m) / jnp.sqrt(v + eps)

def _scatter_add(tgt, idx, src, axis=0):
    return tgt.at[idx].add(src)

def _segment_sum(src, seg, n):
    return jax.ops.segment_sum(src, seg, n)
kernel_name = 'mk_xattn_ffn_d1_seqx_r4_441925'

def setup_inputs(seed: int=0):
    np.random.seed(seed)
    _w = jnp.asarray

    def _rec_inputs():
        import jax
        import jax.numpy as jnp
        _rk = jax.random.key(seed)
        x = 7.22e-05 + 1 * jax.random.normal(jax.random.fold_in(_rk, 1), (2, 1024, 256), jnp.float32)
        _lenS = 1024 - jax.random.randint(jax.random.fold_in(_rk, 7), (2,), 0, max(1, 1024 // 4) + 1, jnp.int32)
        _lenS2 = 64 - jax.random.randint(jax.random.fold_in(_rk, 8), (2,), 0, max(1, 64 // 4) + 1, jnp.int32)
        _ctx_1024P = jax.random.normal(jax.random.fold_in(_rk, 11), (2, 16, 256), jnp.float32)
        _ctx_1024c = jax.random.dirichlet(jax.random.fold_in(_rk, 511), 0.3 * jnp.ones((16,), jnp.float32), (2, 64))
        _ctx_1024t = jnp.einsum('bsk,bkd->bsd', _ctx_1024c, _ctx_1024P)
        _ctx_1024t = _ctx_1024t * jax.lax.rsqrt(jnp.mean(jnp.square(_ctx_1024t)) + 1e-12) * 0.953939
        ctx_1024 = 4.13588e-05 + 0.999923 * (_ctx_1024t + 0.3 * jax.random.normal(jax.random.fold_in(_rk, 611), (2, 64, 256), jnp.float32))
        _validS = jnp.arange(1024)[None, :] < _lenS[:, None]
        _validS2 = jnp.arange(64)[None, :] < _lenS2[:, None]
        _causal = jnp.tril(jnp.ones((1024, 1024), dtype=bool))
        mask_BxSxS2_ik1 = jnp.where(jnp.broadcast_to(_validS2[:, None, :], (2, 1024, 64)), 1, 0).astype(jnp.int32)
        return (x, ctx_1024, mask_BxSxS2_ik1)
    x, ctx_1024, mask_BxSxS2_ik1 = _rec_inputs()

    def _L0_xattn_setup():
        import jax, jax.numpy as jnp
        import numpy as np
        N_HEADS = 16
        D_MODEL = 256
        D_K = D_MODEL // N_HEADS
        B, S = (4, 512)
        NEG_INF = -1000000000.0

        def _proj(x, W, b):
            y = jnp.einsum('bsd,ed->bse', x, W) + b
            Bx, Sx, _ = y.shape
            return y.reshape(Bx, Sx, N_HEADS, D_K).transpose(0, 2, 1, 3)
        key = jax.random.key(seed)
        ks = jax.random.split(key, 12)
        scale = 1.0 / np.sqrt(D_MODEL)
        inp = {'query': jax.random.normal(ks[0], (B, S, D_MODEL), jnp.float32), 'key': jax.random.normal(ks[1], (B, S, D_MODEL), jnp.float32), 'value': jax.random.normal(ks[2], (B, S, D_MODEL), jnp.float32), 'mask': jax.random.randint(ks[3], (B, S, S), 0, 2, jnp.int32), 'Wq': jax.random.normal(ks[4], (D_MODEL, D_MODEL), jnp.float32) * scale, 'bq': jnp.zeros((D_MODEL,), jnp.float32), 'Wk': jax.random.normal(ks[5], (D_MODEL, D_MODEL), jnp.float32) * scale, 'bk': jnp.zeros((D_MODEL,), jnp.float32), 'Wv': jax.random.normal(ks[6], (D_MODEL, D_MODEL), jnp.float32) * scale, 'bv': jnp.zeros((D_MODEL,), jnp.float32), 'Wo': jax.random.normal(ks[7], (D_MODEL, D_MODEL), jnp.float32) * scale, 'bo': jnp.zeros((D_MODEL,), jnp.float32)}
        return inp
    _L0_xattn_all = _L0_xattn_setup()
    _L0_xattn_in = {k: v for k, v in _L0_xattn_all.items() if k in ('Wq', 'bq', 'Wk', 'bk', 'Wv', 'bv', 'Wo', 'bo')}
    del _L0_xattn_all

    def _L0_ffn_setup():
        import jax, jax.numpy as jnp
        import numpy as np
        TAU = 1.0
        K_ROUTE = 3
        EPS = 1e-08

        def _route_combine_weights(x_addr, U, k, tau):
            z = x_addr @ U.T
            topv, topi = jax.lax.top_k(z, k)
            w = jax.nn.softmax(topv / (tau + EPS), axis=1)
            N, L = z.shape
            rows = jnp.arange(N)[:, None]
            return jnp.zeros((N, L), z.dtype).at[rows, topi].add(w)

        def _mixture(inp, C, W):
            L = W.shape[0]
            y = jnp.zeros((inp.shape[0], W.shape[1]), inp.dtype)
            for e in range(L):
                y = y + C[:, e:e + 1] * (inp @ W[e].T)
            return y
        key = jax.random.key(seed)
        ks = jax.random.split(key, 8)
        B, T, D_in, H, D_out, L, d_addr = (8, 2048, 256, 256, 256, 12, 64)

        def unit_rows(k, L_, d_):
            U = jax.random.normal(k, (L_, d_), dtype=jnp.float32)
            U = U - U.mean(axis=1, keepdims=True)
            return U / (jnp.linalg.norm(U, axis=1, keepdims=True) + EPS)

        def norm_tape(k, shape):
            W = jax.random.normal(k, shape, dtype=jnp.float32)
            n = jnp.sqrt(jnp.sum(W * W, axis=tuple(range(1, W.ndim)), keepdims=True)) + 1e-12
            return W / n
        x = jax.random.normal(ks[0], (B, T, D_in), dtype=jnp.float32)
        P_w = jax.random.normal(ks[1], (d_addr, D_in), dtype=jnp.float32) / np.sqrt(D_in)
        U1 = unit_rows(ks[2], L, d_addr)
        U2 = unit_rows(ks[3], L, d_addr)
        U3 = unit_rows(ks[4], L, d_addr)
        W1 = norm_tape(ks[5], (L, H, D_in))
        W2 = norm_tape(ks[6], (L, D_out, H))
        b2 = norm_tape(ks[7], (L, D_out))
        return {'x': x, 'P_w': P_w, 'U1': U1, 'U2': U2, 'U3': U3, 'W1': W1, 'W2': W2, 'b2': b2}
    _L0_ffn_all = _L0_ffn_setup()
    _L0_ffn_in = {k: v for k, v in _L0_ffn_all.items() if k in ('P_w', 'U1', 'U2', 'U3', 'W1', 'W2', 'b2')}
    del _L0_ffn_all
    return {'x': x, 'ctx_1024': ctx_1024, 'mask_BxSxS2_ik1': mask_BxSxS2_ik1, 'L0_xattn_Wq': _L0_xattn_in['Wq'], 'L0_xattn_bq': _L0_xattn_in['bq'], 'L0_xattn_Wk': _L0_xattn_in['Wk'], 'L0_xattn_bk': _L0_xattn_in['bk'], 'L0_xattn_Wv': _L0_xattn_in['Wv'], 'L0_xattn_bv': _L0_xattn_in['bv'], 'L0_xattn_Wo': _L0_xattn_in['Wo'], 'L0_xattn_bo': _L0_xattn_in['bo'], 'L0_ffn_P_w': _L0_ffn_in['P_w'], 'L0_ffn_U1': _L0_ffn_in['U1'], 'L0_ffn_U2': _L0_ffn_in['U2'], 'L0_ffn_U3': _L0_ffn_in['U3'], 'L0_ffn_W1': _L0_ffn_in['W1'], 'L0_ffn_W2': _L0_ffn_in['W2'], 'L0_ffn_b2': _L0_ffn_in['b2']}

def reference(x, ctx_1024, mask_BxSxS2_ik1, L0_xattn_Wq, L0_xattn_bq, L0_xattn_Wk, L0_xattn_bk, L0_xattn_Wv, L0_xattn_bv, L0_xattn_Wo, L0_xattn_bo, L0_ffn_P_w, L0_ffn_U1, L0_ffn_U2, L0_ffn_U3, L0_ffn_W1, L0_ffn_W2, L0_ffn_b2):
    import jax
    import jax.numpy as jnp

    def _L0_xattn_ref(query, key, value, mask, Wq, bq, Wk, bk, Wv, bv, Wo, bo):
        import jax, jax.numpy as jnp
        import numpy as np
        N_HEADS = 16
        D_MODEL = 256
        D_K = D_MODEL // N_HEADS
        B, S = (4, 512)
        NEG_INF = -1000000000.0

        def _proj(x, W, b):
            y = jnp.einsum('bsd,ed->bse', x, W) + b
            Bx, Sx, _ = y.shape
            return y.reshape(Bx, Sx, N_HEADS, D_K).transpose(0, 2, 1, 3)
        q = _proj(query, Wq, bq)
        k = _proj(key, Wk, bk)
        v = _proj(value, Wv, bv)
        scores = jnp.einsum('bhqd,bhkd->bhqk', q, k) / jnp.sqrt(jnp.float32(D_K))
        m = mask[:, None, :, :]
        scores = jnp.where(m == 0, jnp.float32(NEG_INF), scores)
        p_attn = jax.nn.softmax(scores, axis=-1)
        x = jnp.einsum('bhqk,bhkd->bhqd', p_attn, v)
        x = x.transpose(0, 2, 1, 3).reshape(query.shape[0], -1, D_MODEL)
        return jnp.einsum('bsd,ed->bse', x, Wo) + bo

    def _L0_ffn_ref(x, P_w, U1, U2, U3, W1, W2, b2):
        import jax, jax.numpy as jnp
        import numpy as np
        TAU = 1.0
        K_ROUTE = 3
        EPS = 1e-08

        def _route_combine_weights(x_addr, U, k, tau):
            z = x_addr @ U.T
            topv, topi = jax.lax.top_k(z, k)
            w = jax.nn.softmax(topv / (tau + EPS), axis=1)
            N, L = z.shape
            rows = jnp.arange(N)[:, None]
            return jnp.zeros((N, L), z.dtype).at[rows, topi].add(w)

        def _mixture(inp, C, W):
            L = W.shape[0]
            y = jnp.zeros((inp.shape[0], W.shape[1]), inp.dtype)
            for e in range(L):
                y = y + C[:, e:e + 1] * (inp @ W[e].T)
            return y
        B, T, D = x.shape
        xf = x.reshape(B * T, D)
        xa = xf @ P_w.T
        C1 = _route_combine_weights(xa, U1, K_ROUTE, TAU)
        C2 = _route_combine_weights(xa, U2, K_ROUTE, TAU)
        C3 = _route_combine_weights(xa, U3, K_ROUTE, TAU)
        h = jax.nn.gelu(_mixture(xf, C1, W1), approximate=False)
        y = _mixture(h, C2, W2) + C3 @ b2
        return y.reshape(B, T, -1)
    x = x + _L0_xattn_ref(_layernorm(x, axis=-1), ctx_1024, ctx_1024, mask_BxSxS2_ik1, L0_xattn_Wq, L0_xattn_bq, L0_xattn_Wk, L0_xattn_bk, L0_xattn_Wv, L0_xattn_bv, L0_xattn_Wo, L0_xattn_bo)
    x = x + _L0_ffn_ref(_layernorm(x, axis=-1), L0_ffn_P_w, L0_ffn_U1, L0_ffn_U2, L0_ffn_U3, L0_ffn_W1, L0_ffn_W2, L0_ffn_b2)
    return x

_drawn_inputs = setup_inputs


def setup_inputs(seed=0):
    import zlib

    import numpy as np

    out = dict(_drawn_inputs(seed))
    spreads = {'L0_xattn_bq': (0.0, 0.364),
     'L0_xattn_bk': (0.0, 0.8),
     'L0_xattn_bv': (0.0, 0.1),
     'L0_xattn_bo': (0.0, 0.1)}
    factors = {'L0_ffn_U1': 8.0, 'L0_ffn_U2': 8.0, 'L0_ffn_W1': 8.0, 'L0_ffn_W2': 8.0}
    for name, (base, spread) in spreads.items():
        noise = np.random.default_rng([zlib.crc32(name.encode()), seed]).standard_normal(out[name].shape)
        drawn = base * np.exp(spread * noise) if base else spread * noise
        out[name] = jnp.asarray(drawn.astype(out[name].dtype))
    for name, factor in factors.items():
        out[name] = (out[name] * factor).astype(out[name].dtype)
    return out
```

```python
from contextlib import ExitStack

import concourse.bass as bass
from concourse import mybir

ALU = mybir.AluOpType
ACT = mybir.ActivationFunctionType
AX_X = mybir.AxisListType.X
F32 = mybir.dt.float32
F32R = mybir.dt.float32r
I32 = mybir.dt.int32
U32 = mybir.dt.uint32

P = 128
NEG_INF = -1.0e9
LN_EPS = 1e-5
EULER = 2.718281828459045
TOP_K = 3


def xattn_ffn_kernel(nc: bass.Bass, x, mask, ctx_t, wq_t, bq, wk_t, bk, wv_t, bv, wo_t, bo,
                     p_w, u_t, w1_t, w2_t, b2, out):
    BATCH, SEQ, D = x.shape
    KEYS = mask.shape[2]
    HEADS = 16
    DK = D // HEADS
    C = D // P
    TPB = SEQ // P
    T = BATCH * TPB
    EXPERTS = w1_t.shape[1]
    PAIRS = EXPERTS // 2
    ROUTES = 3 * EXPERTS
    HPC = P // DK
    HP = HEADS // 2
    VW = DK + 1
    CHUNKS = 2 * PAIRS
    RING = 3
    SCALE = float(DK) ** -0.5
    assert 2 * KEYS == P and C == 2 and EXPERTS % 2 == 0 and CHUNKS <= T - 1

    def later(t, n):
        return not isinstance(t, int) or t >= n

    def slot1(t):
        return 0 if isinstance(t, int) and t == 0 else 2 * t - 1

    def slot2(t):
        return 2 * T - 1 if isinstance(t, int) and t == T - 1 else 2 * t + 2

    KBD = 5 + 2 * C * BATCH
    SETUP = KBD + 8 + 4 * BATCH + 2
    ROUTE_Z, ROUTE_TOP, ROUTE_EXP, ROUTE_INDEX, ROUTE_STEPS = 1, 4, 5, 8, 14

    with ExitStack() as ctx:
        def sb(name, shape, dt=F32):
            return ctx.enter_context(nc.sbuf_tensor(name, shape, dt))

        def sem(name):
            return ctx.enter_context(nc.semaphore(name))

        x_all = sb("x_all", [P, T, D])
        mask_all = sb("mask_all", [P, T, KEYS], I32)
        ctx_sb = sb("ctx_sb", [P, C, BATCH * KEYS])
        wk_sb = sb("wk_sb", [P, C, D])
        wq_sb = sb("wq_sb", [P, C, D])
        wv_sb = sb("wv_sb", [P, C, D])
        wo_sb = sb("wo_sb", [P, C, D])
        bq_sb = sb("bq_sb", [P, C])
        bk_sb = sb("bk_sb", [P, C])
        bv_sb = sb("bv_sb", [P, D])
        bo_sb = sb("bo_sb", [P, D])
        pw_sb = sb("pw_sb", [p_w.shape[0], D])
        u_sb = sb("u_sb", [p_w.shape[0], ROUTES])
        b2_sb = sb("b2_sb", [EXPERTS, D])
        stage = sb("stage", [P, RING, C, 2 * D])
        ident = sb("ident", [P, P])
        ones = sb("ones", [P, P])
        head_of = sb("head_of", [P, HPC])
        iota_e = sb("iota_e", [P, EXPERTS])
        minus_half = sb("minus_half", [P, 1])
        eps = sb("eps", [P, 1])
        waited = sb("waited", [P, 1])
        euler = sb("euler", [P, 3 * TOP_K])
        neg_all = sb("neg_all", [P, T, KEYS])
        some_key = sb("some_key", [P, T])
        key_max = sb("key_max", [P, T])
        ctx_dup = sb("ctx_dup", [P, C, BATCH, 2, KEYS])
        kt = sb("kt", [P, C, BATCH * KEYS])
        kt_h = sb("kt_h", [P, C, BATCH * KEYS])
        kt_l = sb("kt_l", [P, C, BATCH * KEYS])
        kbd_h = sb("kbd_h", [P, C, BATCH, HPC, KEYS], F32R)
        kbd_l = sb("kbd_l", [P, C, BATCH, HPC, KEYS], F32R)
        v_ext = sb("v_ext", [P, BATCH, HP, 2 * VW])
        wo_h = sb("wo_h", [P, C, D], F32R)
        wo_l = sb("wo_l", [P, C, D], F32R)
        g_h = sb("g_h", [P, C, ROUTES], F32R)
        g_l = sb("g_l", [P, C, ROUTES], F32R)
        w_h = sb("w_h", [P, CHUNKS, C, 2 * D], F32R)
        w_l = sb("w_l", [P, CHUNKS, C, 2 * D], F32R)
        bn = sb("bn", [P, 6])
        mean_var = sb("mean_var", [P, 2])
        var_eps = sb("var_eps", [P, 1])
        rstd = sb("rstd", [P, 1])
        xn = sb("xn", [P, D])
        xn_t = sb("xn_t", [P, C, P])
        q_h = sb("q_h", [P, C, P], F32R)
        q_l = sb("q_l", [P, C, P], F32R)
        s_m = sb("s_m", [P, HEADS, KEYS])
        s_max = sb("s_max", [P, HEADS])
        prob = sb("prob", [P, HEADS, KEYS])
        prob_t = sb("prob_t", [P, HP, P])
        r_sum = sb("r_sum", [P, HEADS])
        a_n = sb("a_n", [P, D])
        a_h = sb("a_h", [P, C, P], F32R)
        a_l = sb("a_l", [P, C, P], F32R)
        xf = sb("xf", [P, D])
        xf_h = sb("xf_h", [P, C, P], F32R)
        xf_l = sb("xf_l", [P, C, P], F32R)
        z_sb = sb("z_sb", [P, 3, EXPERTS])
        top = sb("top", [P, 3, 8])
        top_i = sb("top_i", [P, 3, 8], U32)
        top_d = sb("top_d", [P, 3, TOP_K])
        top_e = sb("top_e", [P, 3 * TOP_K])
        e_sum = sb("e_sum", [P, 3])
        e_rec = sb("e_rec", [P, 3])
        top_w = sb("top_w", [P, 3, TOP_K])
        at_e = sb("at_e", [P, 3, EXPERTS, TOP_K])
        w_at_e = sb("w_at_e", [P, 3, EXPERTS, TOP_K])
        c_new = sb("c_new", [P, 3, EXPERTS])
        c_cur = sb("c_cur", [P, 3, EXPERTS])
        c3_t = sb("c3_t", [EXPERTS, P])
        acc1 = sb("acc1", [P, D])
        acc2 = sb("acc2", [P, D])
        h = sb("h", [P, D])
        h_h = sb("h_h", [P, C, P], F32R)
        h_l = sb("h_l", [P, C, P], F32R)

        banks = ctx.enter_context(nc.psum_tensor("banks", [P, 8, 512], F32))
        ps_s = banks[:, 0:2, :].rearrange("p b (h k) -> p (b h) k", k=KEYS)
        ps_pt = banks[:, 2:4, :].rearrange("p b n -> p (b n)").rearrange("p (j t) -> p j t", t=P)
        ps_v = banks[:, 4, 0:HP * 2 * VW]
        ps_o = banks[:, 4, 0:D]
        ps_x = banks[:, 5, 0:D].rearrange("p (c t) -> p c t", c=C)
        ps_a = banks[:, 6, 0:D].rearrange("p (c t) -> p c t", c=C)
        ps_q = banks[:, 7, 0:D].rearrange("p (c t) -> p c t", c=C)
        ps_t = banks[:, 6, 0:D].rearrange("p (c t) -> p c t", c=C)
        ps_c3 = banks[0:EXPERTS, 7, 0:P]
        ps_y = banks[:, 7, P:P + D]
        ps_z = banks[:, 7, P + D:P + D + ROUTES]

        x_in = [sem(f"x_in{b}") for b in range(BATCH)]
        k_in, q_in, mask_in, v_in, o_in, ffn_in = (sem(n) for n in ("k_in", "q_in", "mask_in", "v_in", "o_in", "ffn_in"))
        w_in = [sem(f"w_in{r}") for r in range(RING)]
        bv_in, bo_in = sem("bv_in"), sem("bo_in")
        consts_set = sem("consts_set")
        setup_dve = sem("setup_dve")
        kt_done, v_done, g_done = sem("kt_done"), sem("v_done"), sem("g_done")
        hi_split = sem("hi_split")
        w_split = sem("w_split")
        var_ready, rstd_ready = sem("var_ready"), sem("rstd_ready")
        xb_ready = sem("xb_ready")
        bn_done, stats_ready, xn_ready = sem("bn_done"), sem("stats_ready"), sem("xn_ready")
        xt_done, xt_copied = sem("xt_done"), sem("xt_copied")
        q_done, q_hi, q_ready = sem("q_done"), sem("q_hi"), sem("q_ready")
        s_done, s_masked, s_maxed, s_ready = sem("s_done"), sem("s_masked"), sem("s_maxed"), sem("s_ready")
        p_ready, pt_done, pt_copied = sem("p_ready"), sem("pt_done"), sem("pt_copied")
        pv_done, sum_rec, a_ready = sem("pv_done"), sem("sum_rec"), sem("a_ready")
        at_done, a_hi, a_lo = sem("at_done"), sem("a_hi"), sem("a_lo")
        o_done, x2_ready = sem("o_done"), sem("x2_ready")
        bn2_done, stats2_ready, xf_ready = sem("bn2_done"), sem("stats2_ready"), sem("xf_ready")
        var2_ready, rstd2_ready = sem("var2_ready"), sem("rstd2_ready")
        xft_done, xf_hi, xf_lo = sem("xft_done"), sem("xf_hi"), sem("xf_lo")
        z_done, route, e_ready = sem("z_done"), sem("route"), sem("e_ready")
        c_moved = sem("c_moved")
        c3t_done, c3t_copied, y_done = sem("c3t_done"), sem("c3t_copied"), sem("y_done")
        y_added = sem("y_added")
        pair_done = sem("pair_done")
        acc = sem("acc")
        h_ready, ht_done, h_hi, h_lo = sem("h_ready"), sem("ht_done"), sem("h_hi"), sem("h_lo")
        stored = sem("stored")

        x_dram = x.rearrange("b (p j) d -> b p j d", j=TPB)
        out_dram = out.rearrange("b (p j) d -> p b j d", j=TPB)
        mask_dram = mask.rearrange("b (p j) k -> b p j k", j=TPB)
        rows = lambda w: w.rearrange("(c p) n -> p c n", c=C)
        w_dram = [w.rearrange("(c p) e o -> p c (e o)", c=C) for w in (w1_t, w2_t)]

        block = ctx.enter_context(nc.Block())

        @block.sync
        def _(sp):
            sp.dma_start(x_all[:, 0:TPB, :], x_dram[0]).then_inc(x_in[0], 16)
            sp.dma_start(ctx_sb[:, :, :], rows(ctx_t)).then_inc(k_in, 16)
            sp.dma_start(wk_sb[:, :, :], rows(wk_t)).then_inc(k_in, 16)
            sp.dma_start(bk_sb[:, :], bk).then_inc(k_in, 16)
            sp.dma_start(wq_sb[:, :, :], rows(wq_t)).then_inc(q_in, 16)
            sp.dma_start(bq_sb[:, :], bq).then_inc(q_in, 16)
            sp.dma_start(x_all[:, TPB:T, :], x_dram[1]).then_inc(x_in[1], 16)
            for b in range(BATCH):
                sp.dma_start(mask_all[:, b * TPB:(b + 1) * TPB, :], mask_dram[b]).then_inc(mask_in, 16)
            sp.dma_start(wv_sb[:, :, :], rows(wv_t)).then_inc(v_in, 16)
            sp.dma_start(bv_sb[:, :], bv.partition_broadcast(P)).then_inc(bv_in, 16)
            sp.dma_start(bo_sb[:, :], bo.partition_broadcast(P)).then_inc(bo_in, 16)
            sp.dma_start(wo_sb[:, :, :], rows(wo_t)).then_inc(o_in, 16)
            sp.dma_start(pw_sb[:, :], p_w).then_inc(ffn_in, 16)
            sp.dma_start(u_sb[:, :], u_t).then_inc(ffn_in, 16)
            sp.dma_start(b2_sb[:, :], b2).then_inc(ffn_in, 16)
            for n in range(CHUNKS):
                layer, pair = n // PAIRS, n % PAIRS
                if n >= RING:
                    sp.wait_ge(w_split, n - RING + 1)
                sp.dma_start(stage[:, n % RING, :, :],
                             w_dram[layer][:, :, pair * 2 * D:(pair + 1) * 2 * D]).then_inc(w_in[n % RING], 16)

            def store(b, j, sums):
                sp.wait_ge(acc, sums)
                sp.dma_start(out_dram[:, b, j, :], x_all[:, j + b * TPB, :]).then_inc(stored, 16)

            for b in range(BATCH):
                with sp.Fori(0, TPB if b < BATCH - 1 else TPB - 1) as j:
                    store(b, j, 2 * EXPERTS * j + (2 * EXPERTS * b * TPB + 3 * EXPERTS))
            store(BATCH - 1, TPB - 1, 2 * EXPERTS * T)
            sp.wait_ge(stored, 16 * T)

        @block.gpsimd
        def _(pool):
            pool.memset(ident[:, :], 0.0).then_inc(consts_set, 1)
            pool.memset(ones[:, :], 1.0).then_inc(consts_set, 1)
            pool.memset(head_of[:, :], 1.0).then_inc(consts_set, 1)
            pool.memset(minus_half[:, :], -0.5).then_inc(consts_set, 1)
            pool.memset(eps[:, :], LN_EPS).then_inc(consts_set, 1)
            pool.memset(euler[:, :], EULER).then_inc(consts_set, 1)
            pool.iota(iota_e[:, :], pattern=[[1, EXPERTS]], base=0, channel_multiplier=0,
                      allow_small_or_imprecise_dtypes=True).then_inc(consts_set, 1)
            pool.wait_ge(consts_set, 7)
            pool.affine_select(out=ident[:, :], in_=ident[:, :], compare_op=ALU.not_equal, fill=1.0, base=0,
                               pattern=[[-1, P]], channel_multiplier=1).then_inc(consts_set, 1)
            pool.affine_select(out=head_of[:, :], in_=head_of[:, :], compare_op=ALU.is_ge, fill=0.0, base=0,
                               pattern=[[-DK, HPC]], channel_multiplier=1).then_inc(consts_set, 1)
            pool.wait_ge(consts_set, 9)
            pool.affine_select(out=head_of[:, :], in_=head_of[:, :], compare_op=ALU.is_ge, fill=0.0, base=DK - 1,
                               pattern=[[DK, HPC]], channel_multiplier=-1).then_inc(consts_set, 1)

            def inverse_deviation(t, stats, var, out_sem):
                pool.wait_ge(stats, t + 1)
                pool.tensor_tensor(var_eps[:, :], mean_var[:, 1:2], eps[:, :], ALU.add).then_inc(var, 1)
                pool.wait_ge(var, t + 1)
                pool.tensor_tensor(rstd[:, :], var_eps[:, :], minus_half[:, :], ALU.pow).then_inc(out_sem, 1)

            def add_output_bias(t):
                pool.wait_ge(xn_ready, t + 1)
                pool.tensor_tensor(x_all[:, t, :], x_all[:, t, :], bo_sb[:, :], ALU.add).then_inc(xb_ready, 1)

            def split_weights(n, slot):
                pool.tensor_copy(w_h[:, n, :, :], stage[:, slot, :, :]).then_inc(hi_split, 1)
                pool.wait_ge(hi_split, n + 1)
                pool.tensor_tensor(w_l[:, n, :, :], stage[:, slot, :, :], w_h[:, n, :, :].bitcast(F32),
                                   ALU.subtract).then_inc(w_split, 1)

            def attention(t):
                inverse_deviation(t, stats_ready, var_ready, rstd_ready)
                add_output_bias(t - 1)

            inverse_deviation(0, stats_ready, var_ready, rstd_ready)
            pool.wait_ge(bo_in, 16)
            attention(1)
            with pool.Fori(0, CHUNKS // RING) as g:
                for r in range(RING):
                    attention(g * RING + (r + 2))
                    pool.wait_ge(w_in[r], g * 16 + 16)
                    split_weights(g * RING + r, r)
            for t in range(CHUNKS + 2, T):
                attention(t)
            add_output_bias(T - 1)

            def exponentials(t):
                pool.wait_ge(route, ROUTE_STEPS * t + ROUTE_EXP)
                pool.tensor_tensor(top_e[:, :], euler[:, :], top_d[:, :, :].rearrange("p r k -> p (r k)"),
                                   ALU.pow).then_inc(e_ready, 1)

            inverse_deviation(0, stats2_ready, var2_ready, rstd2_ready)
            exponentials(0)
            with pool.Fori(1, T) as t:
                inverse_deviation(t, stats2_ready, var2_ready, rstd2_ready)
                exponentials(t)


        @block.scalar
        def _(act):
            def copy_xt(t):
                act.wait_ge(xt_done, t + 1)
                if later(t, 1):
                    act.wait_ge(q_done, t)
                nc.scalar.activation(xn_t[:, :, :], ps_x, ACT.Copy).then_inc(xt_copied, 1)

            def q_high(t):
                act.wait_ge(q_done, t + 1)
                if later(t, 1):
                    act.wait_ge(s_done, t)
                for c in range(C):
                    nc.scalar.activation(q_h[:, c, :], ps_q[:, c, :], ACT.Identity,
                                         bias=bq_sb[:, c:c + 1]).then_inc(q_hi, 1)

            def exp_scores(t):
                act.wait_ge(s_ready, t + 1)
                if later(t, 1):
                    act.wait_ge(pt_done, 2 * t)
                nc.scalar.activation(prob[:, :, :], s_m[:, :, :], ACT.Exp).then_inc(p_ready, 1)

            def copy_pt(t):
                if later(t, 1):
                    act.wait_ge(pv_done, t)
                for half in range(2):
                    act.wait_ge(pt_done, 2 * t + half + 1)
                    j = half * HP // 2
                    nc.scalar.activation(prob_t[:, j:j + HP // 2, :], ps_pt[:, j:j + HP // 2, :],
                                         ACT.Copy).then_inc(pt_copied, 1)

            def a_high(t):
                act.wait_ge(at_done, t + 1)
                if later(t, 1):
                    act.wait_ge(o_done, t)
                nc.scalar.activation(a_h[:, :, :], ps_a, ACT.Copy).then_inc(a_hi, 1)

            act.wait_ge(q_in, 32)
            copy_xt(0)
            q_high(0)
            copy_xt(1)
            q_high(1)
            exp_scores(0)
            copy_xt(2)

            def attention(t):
                copy_pt(t)
                a_high(t)
                q_high(t + 2)
                exp_scores(t + 1)

            attention(0)
            copy_xt(3)
            with act.Fori(1, T - 3) as t:
                attention(t)
                copy_xt(t + 3)
            attention(T - 3)
            copy_pt(T - 2)
            a_high(T - 2)
            exp_scores(T - 1)
            copy_pt(T - 1)
            a_high(T - 1)

            def xf_high(t):
                act.wait_ge(xft_done, t + 1)
                nc.scalar.activation(xf_h[:, :, :], ps_t, ACT.Copy).then_inc(xf_hi, 1)

            def h_high(t):
                act.wait_ge(ht_done, t + 1)
                nc.scalar.activation(h_h[:, :, :], ps_t, ACT.Copy).then_inc(h_hi, 1)

            def copy_c3t(t):
                act.wait_ge(c3t_done, t + 1)
                nc.scalar.activation(c3_t[:, :], ps_c3, ACT.Copy).then_inc(c3t_copied, 1)

            def gelu(t, acc_count):
                act.wait_ge(acc, acc_count)
                if later(t, 1):
                    act.wait_ge(ht_done, t)
                nc.scalar.activation(h[:, :], acc1[:, :], ACT.Gelu).then_inc(h_ready, 1)

            xf_high(0)
            gelu(0, EXPERTS)
            xf_high(1)

            def experts(t):
                h_high(t)
                copy_c3t(t)
                gelu(t + 1, EXPERTS * 2 * (t + 1))
                xf_high(t + 2)

            experts(0)
            with act.Fori(1, T - 2) as t:
                experts(t)
            h_high(T - 2)
            copy_c3t(T - 2)
            gelu(T - 1, EXPERTS * 2 * (T - 1))
            h_high(T - 1)
            copy_c3t(T - 1)

        @block.vector
        def _(dve):
            def statistics(t, src, done, ready):
                dve.bn_stats(bn[:, :], src[:, t, :]).then_inc(done, 1)
                dve.wait_ge(done, t + 1)
                dve.memset(waited[:, :], 0.0)
                dve.bn_aggr(mean_var[:, :], bn[:, :]).then_inc(ready, 1)

            def normalise(t, src, dst, rstd_sem, ready):
                dve.wait_ge(rstd_sem, t + 1)
                dve.tensor_scalar(dst[:, :], src[:, t, :], mean_var[:, 0:1], rstd[:, 0:1],
                                  ALU.subtract, ALU.mult).then_inc(ready, 1)

            def stats1(t):
                statistics(t, x_all, bn_done, stats_ready)

            def normalise1(t):
                if later(t, 1):
                    dve.wait_ge(xt_done, t)
                normalise(t, x_all, xn, rstd_ready, xn_ready)

            def normalise2(t):
                dve.wait_ge(xft_done, t)
                normalise(t, x_all, xf, rstd2_ready, xf_ready)

            def q_low(t):
                dve.wait_ge(q_hi, C * t + C)
                if later(t, 1):
                    dve.wait_ge(s_done, t)
                for c in range(C):
                    ins = dve.scalar_tensor_tensor(out=q_l[:, c, :], in0=ps_q[:, c, :], scalar=bq_sb[:, c:c + 1],
                                                   in1=q_h[:, c, :].bitcast(F32), op0=ALU.add, op1=ALU.subtract)
                ins.then_inc(q_ready, 1)

            def mask_scores(t):
                dve.wait_ge(s_done, t + 1)
                if later(t, 1):
                    dve.wait_ge(p_ready, t)
                dve.scalar_tensor_tensor(out=s_m[:, :, :], in0=ps_s, scalar=some_key[:, bass.ds(t, 1)],
                                         in1=neg_all[:, t, :].unsqueeze(1).to_broadcast([P, HEADS, KEYS]),
                                         op0=ALU.mult, op1=ALU.add).then_inc(s_masked, 1)

            def max_scores(t):
                dve.wait_ge(s_masked, t + 1)
                dve.tensor_reduce(s_max[:, :], s_m[:, :, :], AX_X, ALU.max).then_inc(s_maxed, 1)

            def subtract_max(t):
                dve.wait_ge(s_maxed, t + 1)
                dve.tensor_tensor(s_m[:, :, :], s_m[:, :, :],
                                  s_max[:, :].unsqueeze(2).to_broadcast([P, HEADS, KEYS]),
                                  ALU.subtract).then_inc(s_ready, 1)

            def divide_by_sum(t):
                dve.wait_ge(pv_done, t + 1)
                pv = ps_v.rearrange("p (h v) -> p h v", v=VW)
                dve.reciprocal(r_sum[:, :], pv[:, :, DK]).then_inc(sum_rec, 1)
                dve.wait_ge(sum_rec, t + 1)
                if later(t, 1):
                    dve.wait_ge(at_done, t)
                dve.tensor_tensor(a_n[:, :].rearrange("p (h v) -> p h v", v=DK), pv[:, :, 0:DK],
                                  r_sum[:, :].unsqueeze(2).to_broadcast([P, HEADS, DK]),
                                  ALU.mult).then_inc(a_ready, 1)

            def a_low(t):
                dve.wait_ge(a_hi, t + 1)
                if later(t, 1):
                    dve.wait_ge(o_done, t)
                dve.tensor_tensor(a_l[:, :, :], ps_a, a_h[:, :, :].bitcast(F32), ALU.subtract).then_inc(a_lo, 1)

            def add_attention(t):
                dve.wait_ge(o_done, t + 1)
                dve.wait_ge(xb_ready, t + 1)
                dve.tensor_tensor(x_all[:, t, :], ps_o, x_all[:, t, :], ALU.add).then_inc(x2_ready, 1)

            dve.wait_ge(x_in[0], 16)
            stats1(0)
            normalise1(0)
            stats1(1)
            dve.wait_ge(k_in, 48)
            dve.tensor_copy(ctx_dup[:, :, :, :, :],
                            ctx_sb[:, :, :].rearrange("p c (b k) -> p (c b) k", b=BATCH).unsqueeze(2)
                            .to_broadcast([P, C * BATCH, 2, KEYS])).then_inc(setup_dve, 1)
            dve.wait_ge(kt_done, 1)
            for c in range(C):
                dve.tensor_scalar(kt[:, c, :], banks[:, 0, c * P:(c + 1) * P], bk_sb[:, c:c + 1], None,
                                  ALU.add).then_inc(setup_dve, 1)
            dve.wait_ge(setup_dve, 3)
            dve.tensor_copy(kt_h[:, :, :].bitcast(F32R), kt[:, :, :]).then_inc(setup_dve, 1)
            dve.wait_ge(setup_dve, 4)
            dve.tensor_tensor(kt_l[:, :, :], kt[:, :, :], kt_h[:, :, :], ALU.subtract).then_inc(setup_dve, 1)
            dve.wait_ge(setup_dve, 5)
            dve.wait_ge(consts_set, 10)
            for b in range(BATCH):
                for c in range(C):
                    for dst, src in ((kbd_h, kt_h), (kbd_l, kt_l)):
                        dve.tensor_tensor(dst[:, c, b, :, :],
                                          src[:, c, b * KEYS:(b + 1) * KEYS].unsqueeze(1).to_broadcast([P, HPC, KEYS]),
                                          head_of[:, :].unsqueeze(2).to_broadcast([P, HPC, KEYS]),
                                          ALU.mult).then_inc(setup_dve, 1)
            dve.wait_ge(mask_in, 32)
            dve.tensor_scalar(neg_all[:, :, :], mask_all[:, :, :], 0, NEG_INF, ALU.is_equal,
                              ALU.mult).then_inc(setup_dve, 1)
            dve.wait_ge(setup_dve, KBD + 1)
            dve.tensor_reduce(key_max[:, :], neg_all[:, :, :], AX_X, ALU.max).then_inc(setup_dve, 1)
            dve.wait_ge(setup_dve, KBD + 2)
            dve.tensor_scalar(some_key[:, :], key_max[:, :], NEG_INF / 2, SCALE, ALU.is_gt,
                              ALU.mult).then_inc(setup_dve, 1)
            q_low(0)
            normalise1(1)
            stats1(2)
            dve.memset(v_ext[:, :, :, :], 0.0).then_inc(setup_dve, 1)
            dve.wait_ge(setup_dve, KBD + 4)
            dve.wait_ge(bv_in, 16)
            dve.wait_ge(v_done, 1)
            for b in range(BATCH):
                for side in range(2):
                    r = slice(side * KEYS, (side + 1) * KEYS)
                    v = banks[r, 2 + b, 0:D].rearrange("p (j s v) -> p j s v", s=2, v=DK)[:, :, side, :]
                    bias = bv_sb[r, :].rearrange("p (j s v) -> p j s v", s=2, v=DK)[:, :, side, :]
                    dve.tensor_tensor(v_ext[r, b, :, side * VW:side * VW + DK], v, bias,
                                      ALU.add).then_inc(setup_dve, 1)
                    dve.memset(v_ext[r, b, :, side * VW + DK], 1.0).then_inc(setup_dve, 1)

            mask_scores(0)
            max_scores(0)
            subtract_max(0)
            q_low(1)
            normalise1(2)
            dve.wait_ge(o_in, 16)
            dve.tensor_copy(wo_h[:, :, :], wo_sb[:, :, :]).then_inc(setup_dve, 1)
            dve.wait_ge(setup_dve, KBD + 13)
            dve.tensor_tensor(wo_l[:, :, :], wo_sb[:, :, :], wo_h[:, :, :].bitcast(F32),
                              ALU.subtract).then_inc(setup_dve, 1)
            dve.wait_ge(g_done, 1)
            for c in range(C):
                dve.tensor_copy(g_h[:, c, :], banks[:, 4, c * ROUTES:(c + 1) * ROUTES]).then_inc(setup_dve, 1)
            dve.wait_ge(setup_dve, KBD + 16)
            for c in range(C):
                dve.tensor_tensor(g_l[:, c, :], banks[:, 4, c * ROUTES:(c + 1) * ROUTES], g_h[:, c, :].bitcast(F32),
                                  ALU.subtract).then_inc(setup_dve, 1)

            def attention(t):
                mask_scores(t + 1)
                max_scores(t + 1)
                divide_by_sum(t)
                subtract_max(t + 1)
                a_low(t)
                q_low(t + 2)
                add_attention(t)

            stats1(3)
            attention(0)
            normalise1(3)
            dve.wait_ge(x_in[1], 16)
            with dve.Fori(1, T - 3) as t:
                stats1(t + 3)
                attention(t)
                normalise1(t + 3)
            attention(T - 3)
            mask_scores(T - 1)
            max_scores(T - 1)
            divide_by_sum(T - 2)
            subtract_max(T - 1)
            a_low(T - 2)
            add_attention(T - 2)
            divide_by_sum(T - 1)
            a_low(T - 1)
            add_attention(T - 1)

            def xf_low(t):
                dve.wait_ge(xf_hi, t + 1)
                dve.tensor_tensor(xf_l[:, :, :], ps_t, xf_h[:, :, :].bitcast(F32), ALU.subtract).then_inc(xf_lo, 1)

            def h_low(t):
                dve.wait_ge(h_hi, t + 1)
                dve.tensor_tensor(h_l[:, :, :], ps_t, h_h[:, :, :].bitcast(F32), ALU.subtract).then_inc(h_lo, 1)

            def find_top(t):
                n = ROUTE_STEPS * t
                dve.wait_ge(z_done, t + 1)
                dve.tensor_copy(z_sb[:, :, :].rearrange("p r e -> p (r e)"), ps_z).then_inc(route, 1)
                dve.wait_ge(route, n + ROUTE_Z)
                dve.memset(waited[:, :], 0.0)
                for r in range(3):
                    dve.max(top[:, r, :], z_sb[:, r, :]).then_inc(route, 1)
                dve.wait_ge(route, n + ROUTE_TOP)
                if later(t, 1):
                    dve.wait_ge(e_ready, t)
                dve.tensor_tensor(top_d[:, :, :], top[:, :, 0:TOP_K],
                                  top[:, :, 0:1].to_broadcast([P, 3, TOP_K]), ALU.subtract).then_inc(route, 1)
                for r in range(3):
                    dve.max_index(top_i[:, r, :], top[:, r, :], z_sb[:, r, :]).then_inc(route, 1)

            def combine_weights(t):
                n = ROUTE_STEPS * t + ROUTE_INDEX
                dve.wait_ge(route, n)
                dve.tensor_tensor(at_e[:, :, :, :],
                                  top_i[:, :, 0:TOP_K].unsqueeze(2).to_broadcast([P, 3, EXPERTS, TOP_K]),
                                  iota_e[:, :].unsqueeze(1).unsqueeze(3).to_broadcast([P, 3, EXPERTS, TOP_K]),
                                  ALU.is_equal).then_inc(route, 1)
                dve.wait_ge(e_ready, t + 1)
                e = top_e[:, :].rearrange("p (r k) -> p r k", r=3)
                dve.tensor_reduce(e_sum[:, :], e, AX_X, ALU.add).then_inc(route, 1)
                dve.wait_ge(route, n + 2)
                dve.reciprocal(e_rec[:, :], e_sum[:, :]).then_inc(route, 1)
                dve.wait_ge(route, n + 3)
                dve.tensor_tensor(top_w[:, :, :], e, e_rec[:, :].unsqueeze(2).to_broadcast([P, 3, TOP_K]),
                                  ALU.mult).then_inc(route, 1)
                dve.wait_ge(route, n + 4)
                dve.tensor_tensor(w_at_e[:, :, :, :], at_e[:, :, :, :],
                                  top_w[:, :, :].unsqueeze(2).to_broadcast([P, 3, EXPERTS, TOP_K]),
                                  ALU.mult).then_inc(route, 1)
                dve.wait_ge(route, n + 5)
                if later(t, 1):
                    dve.wait_ge(c_moved, t)
                dve.tensor_reduce(c_new[:, :, :], w_at_e[:, :, :, :], AX_X, ALU.add).then_inc(route, 1)

            def move_weights(t):
                dve.wait_ge(route, ROUTE_STEPS * (t + 1))
                if later(t, 1):
                    dve.wait_ge(c3t_done, t)
                    dve.wait_ge(acc, EXPERTS * (2 * t + 1))
                dve.tensor_copy(c_cur[:, :, :], c_new[:, :, :]).then_inc(c_moved, 1)

            def sum_pair(slot, pair, weights, total, last=None):
                dve.wait_ge(pair_done, PAIRS * slot + pair + 1)
                for e in (2 * pair, 2 * pair + 1):
                    product = banks[:, pair, (e % 2) * D:(e % 2 + 1) * D]
                    if e == 0 and total is acc1:
                        dve.tensor_scalar(total[:, :], product, weights[:, e:e + 1], None,
                                          ALU.mult).then_inc(acc, 1)
                        continue
                    if e > 0:
                        dve.wait_ge(acc, EXPERTS * slot + e)
                    dst = last if e == EXPERTS - 1 and last is not None else total[:, :]
                    dve.scalar_tensor_tensor(out=dst, in0=product, scalar=weights[:, e:e + 1], in1=total[:, :],
                                             op0=ALU.mult, op1=ALU.add).then_inc(acc, 1)

            def layer1_pairs(t, pairs):
                for pair in pairs:
                    if pair == 0:
                        dve.wait_ge(route, ROUTE_STEPS * (t + 1))
                    if pair == 0 and later(t, 1):
                        dve.wait_ge(h_ready, t)
                    sum_pair(slot1(t), pair, c_new[:, 0, :], acc1)

            def start_layer2(t):
                dve.wait_ge(y_done, t + 1)
                dve.tensor_tensor(acc2[:, :], ps_y, x_all[:, t, :], ALU.add).then_inc(y_added, 1)
                dve.wait_ge(y_added, t + 1)
                dve.wait_ge(c_moved, t + 1)

            def layer2_pairs(t, pairs):
                for pair in pairs:
                    sum_pair(slot2(t), pair, c_cur[:, 1, :], acc2, x_all[:, t, :])

            statistics(0, x_all, bn2_done, stats2_ready)
            normalise(0, x_all, xf, rstd2_ready, xf_ready)
            xf_low(0)
            statistics(1, x_all, bn2_done, stats2_ready)
            find_top(0)
            combine_weights(0)
            normalise2(1)
            layer1_pairs(0, range(PAIRS))
            xf_low(1)
            find_top(1)
            move_weights(0)
            combine_weights(1)

            def experts(t, ahead=True):
                if ahead:
                    statistics(t + 2, x_all, bn2_done, stats2_ready)
                layer1_pairs(t + 1, range(0, 4))
                h_low(t)
                layer1_pairs(t + 1, range(4, PAIRS))
                start_layer2(t)
                layer2_pairs(t, range(0, 1))
                if ahead:
                    normalise2(t + 2)
                layer2_pairs(t, range(1, 4))
                if ahead:
                    xf_low(t + 2)
                layer2_pairs(t, range(4, 5))
                if ahead:
                    find_top(t + 2)
                layer2_pairs(t, range(5, PAIRS))
                move_weights(t + 1)
                if ahead:
                    combine_weights(t + 2)

            experts(0)
            with dve.Fori(1, T - 2) as t:
                experts(t)
            experts(T - 2, ahead=False)
            h_low(T - 1)
            start_layer2(T - 1)
            layer2_pairs(T - 1, range(PAIRS))

        @block.tensor
        def _(pe):
            def split_product(dst, left, right):
                (lh, ll), (rh, rl) = left, right
                terms = [(c, a, b) for c in range(C) for a, b in ((lh, rh), (ll, rh), (lh, rl))]
                for i, (c, a, b) in enumerate(terms):
                    ins = pe.matmul(dst, a(c), b(c), start=(i == 0), stop=(i == len(terms) - 1))
                return ins

            def whole(w):
                return lambda c: w[:, c, :]

            def keys_project():
                pe.wait_ge(k_in, 48)
                for m in range(C):
                    for c in range(C):
                        ins = pe.matmul(banks[:, 0, m * P:(m + 1) * P], wk_sb[:, c, m * P:(m + 1) * P],
                                        ctx_sb[:, c, :], start=(c == 0), stop=(c == C - 1))
                ins.then_inc(kt_done, 1)

            def values_project():
                pe.wait_ge(v_in, 16)
                pe.wait_ge(setup_dve, 1)
                for b in range(BATCH):
                    for c in range(C):
                        ins = pe.matmul(banks[:, 2 + b, 0:D], ctx_dup[:, c, b, :, :].rearrange("p s k -> p (s k)"),
                                        wv_sb[:, c, :], start=(c == 0), stop=(c == C - 1))
                ins.then_inc(v_done, 1)

            def router_weights():
                pe.wait_ge(ffn_in, 48)
                for c in range(C):
                    ins = pe.matmul(banks[:, 4, c * ROUTES:(c + 1) * ROUTES], pw_sb[:, c * P:(c + 1) * P],
                                    u_sb[:, :], start=True, stop=True)
                ins.then_inc(g_done, 1)

            def transpose_x(t):
                pe.wait_ge(xn_ready, t + 1)
                if later(t, 1):
                    pe.wait_ge(xt_copied, t)
                for c in range(C):
                    ins = pe.transpose(ps_x[:, c, :], xn[:, c * P:(c + 1) * P], ident[:, :])
                ins.then_inc(xt_done, 1)

            def queries(t):
                pe.wait_ge(xt_copied, t + 1)
                if later(t, 1):
                    pe.wait_ge(q_ready, t)
                for m in range(C):
                    for c in range(C):
                        ins = pe.matmul(ps_q[:, m, :], wq_sb[:, c, m * P:(m + 1) * P], xn_t[:, c, :],
                                        start=(c == 0), stop=(c == C - 1))
                ins.then_inc(q_done, 1)

            def scores(t, b):
                pe.wait_ge(q_ready, t + 1)
                if later(t, 1):
                    pe.wait_ge(s_masked, t)
                for c in range(C):
                    kh = kbd_h[:, c, b, :, :].rearrange("p h k -> p (h k)")
                    kl = kbd_l[:, c, b, :, :].rearrange("p h k -> p (h k)")
                    pe.matmul(banks[:, c, :], q_h[:, c, :], kh, start=True, stop=False)
                    pe.matmul(banks[:, c, :], q_l[:, c, :], kh, start=False, stop=False)
                    ins = pe.matmul(banks[:, c, :], q_h[:, c, :], kl, start=False, stop=True)
                ins.then_inc(s_done, 1)

            def transpose_probs(t):
                pe.wait_ge(p_ready, t + 1)
                if later(t, 1):
                    pe.wait_ge(pt_copied, 2 * t)
                for half in range(2):
                    for j in range(half * HP // 2, (half + 1) * HP // 2):
                        ins = pe.transpose(ps_pt[:, j, :], prob[:, 2 * j:2 * j + 2, :].rearrange("p h k -> p (h k)"),
                                           ident[:, :])
                    ins.then_inc(pt_done, 1)

            def weigh_values(t, b):
                if later(t, 1):
                    pe.wait_ge(x2_ready, t)
                for half in range(2):
                    pe.wait_ge(pt_copied, 2 * t + half + 1)
                    for j in range(half * HP // 2, (half + 1) * HP // 2):
                        ins = pe.matmul(ps_v[:, j * 2 * VW:(j + 1) * 2 * VW], prob_t[:, j, :], v_ext[:, b, j, :],
                                        start=True, stop=True)
                ins.then_inc(pv_done, 1)

            def transpose_a(t):
                pe.wait_ge(a_ready, t + 1)
                if later(t, 1):
                    pe.wait_ge(a_lo, t)
                for c in range(C):
                    ins = pe.transpose(ps_a[:, c, :], a_n[:, c * P:(c + 1) * P], ident[:, :])
                ins.then_inc(at_done, 1)

            def output_project(t):
                pe.wait_ge(a_lo, t + 1)
                split_product(ps_o, (whole(a_h), whole(a_l)), (whole(wo_h), whole(wo_l))).then_inc(o_done, 1)

            pe.wait_ge(consts_set, 10)
            transpose_x(0)
            keys_project()
            pe.wait_ge(q_in, 32)
            queries(0)
            transpose_x(1)
            values_project()
            pe.wait_ge(setup_dve, KBD)
            scores(0, 0)
            queries(1)
            transpose_x(2)
            router_weights()

            def attention(t, b, b_next):
                scores(t + 1, b_next)
                transpose_probs(t)
                weigh_values(t, b)
                transpose_a(t)
                queries(t + 2)
                output_project(t)

            pe.wait_ge(setup_dve, SETUP)
            attention(0, 0, 0)
            transpose_x(3)
            with pe.Fori(1, T - 3) as t:
                attention(t, t // TPB, (t + 1) // TPB)
                transpose_x(t + 3)
            attention(T - 3, BATCH - 1, BATCH - 1)
            scores(T - 1, BATCH - 1)
            for t in (T - 2, T - 1):
                transpose_probs(t)
                weigh_values(t, BATCH - 1)
                transpose_a(t)
                output_project(t)

            def transpose_xf(t):
                pe.wait_ge(xf_ready, t + 1)
                if later(t, 2):
                    pe.wait_ge(h_lo, t - 1)
                elif t == 1:
                    pe.wait_ge(xf_lo, 1)
                for c in range(C):
                    ins = pe.transpose(ps_t[:, c, :], xf[:, c * P:(c + 1) * P], ident[:, :])
                ins.then_inc(xft_done, 1)

            def logits(t):
                pe.wait_ge(xf_lo, t + 1)
                if later(t, 2):
                    pe.wait_ge(y_added, t - 1)
                elif t == 1:
                    pe.wait_ge(route, ROUTE_Z)
                split_product(ps_z, (whole(xf_h), whole(xf_l)), (whole(g_h), whole(g_l))).then_inc(z_done, 1)

            def transpose_h(t):
                pe.wait_ge(h_ready, t + 1)
                pe.wait_ge(xf_lo, min(t + 2, T) if isinstance(t, int) else t + 2)
                for c in range(C):
                    ins = pe.transpose(ps_t[:, c, :], h[:, c * P:(c + 1) * P], ident[:, :])
                ins.then_inc(ht_done, 1)

            def transpose_c3(t):
                pe.wait_ge(c_moved, t + 1)
                if later(t, 1):
                    pe.wait_ge(y_added, t)
                pe.transpose(ps_c3, c_cur[:, 2, :], ident[:, :]).then_inc(c3t_done, 1)

            def expert_bias(t):
                pe.wait_ge(c3t_copied, t + 1)
                pe.matmul(ps_y, c3_t[:, :], b2_sb[:, :], start=True, stop=True).then_inc(y_done, 1)

            def expert_pairs(slot, pairs, left, layer):
                for pair in pairs:
                    if later(slot, 1):
                        pe.wait_ge(acc, EXPERTS * slot - EXPERTS + 2 * pair + 2)
                    n = layer * PAIRS + pair
                    split_product(banks[:, pair, :], left,
                                  (lambda c: w_h[:, n, c, :], lambda c: w_l[:, n, c, :])).then_inc(pair_done, 1)

            xf_parts, h_parts = (whole(xf_h), whole(xf_l)), (whole(h_h), whole(h_l))

            pe.wait_ge(x2_ready, T)
            transpose_xf(0)
            logits(0)
            pe.wait_ge(w_split, PAIRS)
            expert_pairs(0, range(0, 3), xf_parts, 0)
            expert_pairs(0, range(3, PAIRS), xf_parts, 0)
            transpose_xf(1)
            logits(1)
            pe.wait_ge(w_split, CHUNKS)

            def experts(t, ahead=True):
                expert_pairs(slot1(t + 1), range(0, 3), xf_parts, 0)
                transpose_h(t)
                transpose_c3(t)
                expert_pairs(slot1(t + 1), range(3, PAIRS), xf_parts, 0)
                expert_bias(t)
                pe.wait_ge(h_lo, t + 1)
                expert_pairs(slot2(t), range(0, 2), h_parts, 1)
                if ahead:
                    transpose_xf(t + 2)
                expert_pairs(slot2(t), range(2, 4), h_parts, 1)
                if ahead:
                    logits(t + 2)
                expert_pairs(slot2(t), range(4, PAIRS), h_parts, 1)

            experts(0)
            with pe.Fori(1, T - 2) as t:
                experts(t)
            experts(T - 2, ahead=False)
            transpose_h(T - 1)
            transpose_c3(T - 1)
            expert_bias(T - 1)
            pe.wait_ge(h_lo, T)
            expert_pairs(2 * T - 1, range(PAIRS), h_parts, 1)


_INS = ["x", "mask", "ctx_t", "wq_t", "bq", "wk_t", "bk", "wv_t", "bv", "wo_t", "bo", "p_w", "u_t", "w1_t", "w2_t", "b2"]
_OUTS = [((2, 1024, 256), "float32")]


def kernel(x, ctx_1024, mask_BxSxS2_ik1, L0_xattn_Wq, L0_xattn_bq, L0_xattn_Wk, L0_xattn_bk, L0_xattn_Wv,
           L0_xattn_bv, L0_xattn_Wo, L0_xattn_bo, L0_ffn_P_w, L0_ffn_U1, L0_ffn_U2, L0_ffn_U3, L0_ffn_W1,
           L0_ffn_W2, L0_ffn_b2):
    import numpy as _np
    import concourse.bacc as _bacc
    from concourse import mybir as _mybir
    from concourse.bass_utils import run_bass_kernel_spmd as _run

    d = x.shape[-1]
    columns = lambda v: _np.asarray(v).reshape(-1, P).T
    laid_out = {
        "x": x, "mask": mask_BxSxS2_ik1,
        "ctx_t": _np.asarray(ctx_1024).reshape(-1, d).T,
        "wq_t": _np.asarray(L0_xattn_Wq).T, "bq": columns(L0_xattn_bq),
        "wk_t": _np.asarray(L0_xattn_Wk).T, "bk": columns(L0_xattn_bk),
        "wv_t": _np.asarray(L0_xattn_Wv).T, "bv": _np.asarray(L0_xattn_bv),
        "wo_t": _np.asarray(L0_xattn_Wo).T, "bo": _np.asarray(L0_xattn_bo),
        "p_w": L0_ffn_P_w,
        "u_t": _np.concatenate([_np.asarray(u) for u in (L0_ffn_U1, L0_ffn_U2, L0_ffn_U3)], axis=0).T,
        "w1_t": _np.asarray(L0_ffn_W1).transpose(2, 0, 1), "w2_t": _np.asarray(L0_ffn_W2).transpose(2, 0, 1),
        "b2": L0_ffn_b2,
    }
    nc = _bacc.Bacc("TRN2", target_bir_lowering=False, num_devices=1)
    arrays, args = {}, []
    for name in _INS:
        a = _np.ascontiguousarray(laid_out[name])
        arrays[f"in_{name}_dram"] = a
        args.append(nc.dram_tensor(f"in_{name}_dram", a.shape, _mybir.dt.from_np(a.dtype), kind="ExternalInput").ap())
    for i, (shape, dtype) in enumerate(_OUTS):
        dt = _mybir.dt.from_np(_np.dtype(dtype))
        args.append(nc.dram_tensor(f"out_{i}_dram", shape, dt, kind="ExternalOutput").ap())
    xattn_ffn_kernel(nc, *args)
    r = _run(nc, [arrays], core_ids=[0])
    return r.results[0]["out_0_dram"]
```

```python
from contextlib import ExitStack

import concourse.bass as bass
from concourse import mybir

ALU = mybir.AluOpType
ACT = mybir.ActivationFunctionType
AX_X = mybir.AxisListType.X
F32 = mybir.dt.float32
F32R = mybir.dt.float32r
BF16 = mybir.dt.bfloat16
I32 = mybir.dt.int32
U32 = mybir.dt.uint32

P = 128
MASKED = -2.0 ** 99
LN_EPS = 1e-5
EULER = 2.718281828459045
TOP_K = 3


def xattn_ffn_kernel(nc: bass.Bass, x, mask, ctx_t, wq_t, bq, wk_t, bk, wv_t, bv, wo_t, bo,
                     p_w, u_t, w1_t, w2_t, b2, out):
    BATCH, SEQ, D = x.shape
    KEYS = mask.shape[2]
    HEADS = 16
    DK = D // HEADS
    C = D // P
    TPB = SEQ // P
    T = BATCH * TPB
    EXPERTS = w1_t.shape[1]
    PAIRS = EXPERTS // 2
    ROUTES = 3 * EXPERTS
    HPC = P // DK
    HP = HEADS // 2
    VW = DK + 1
    CHUNKS = 2 * PAIRS
    RING = 3
    SCALE = float(DK) ** -0.5
    assert 2 * KEYS == P and C == 2 and EXPERTS % 2 == 0 and CHUNKS == T - 4

    def later(t, n):
        return not isinstance(t, int) or t >= n

    def slot1(t):
        return 0 if isinstance(t, int) and t == 0 else 2 * t - 1

    def slot2(t):
        return 2 * T - 1 if isinstance(t, int) and t == T - 1 else 2 * t + 2

    KBD = 5 + 2 * C * BATCH
    SETUP = KBD + 9 + 4 * BATCH
    SUMS = EXPERTS + 1
    BANK = (0, 1, 2, 3, 4, 6)
    ROUTE_Z, ROUTE_TOP, ROUTE_EXP, ROUTE_INDEX, ROUTE_STEPS = 1, 4, 5, 8, 14

    with ExitStack() as ctx:
        def sb(name, shape, dt=F32):
            return ctx.enter_context(nc.sbuf_tensor(name, shape, dt))

        def sem(name):
            return ctx.enter_context(nc.semaphore(name))

        x_all = sb("x_all", [P, T, D])
        mask_all = sb("mask_all", [P, T, KEYS], I32)
        ctx_sb = sb("ctx_sb", [P, C, BATCH * KEYS])
        wk_sb = sb("wk_sb", [P, C, D])
        wq_sb = sb("wq_sb", [P, C, D])
        wv_sb = sb("wv_sb", [P, C, D])
        wo_sb = sb("wo_sb", [P, C, D])
        bq_sb = sb("bq_sb", [P, C])
        bk_sb = sb("bk_sb", [P, C])
        bv_sb = sb("bv_sb", [P, D])
        bo_sb = sb("bo_sb", [P, D])
        pw_sb = sb("pw_sb", [p_w.shape[0], D])
        u_sb = sb("u_sb", [p_w.shape[0], ROUTES])
        b2_sb = sb("b2_sb", [EXPERTS, D])
        stage = sb("stage", [P, RING, C, 2 * D])
        ident = sb("ident", [P, P])
        ones = sb("ones", [P, P])
        head_of = sb("head_of", [P, HPC])
        iota_e = sb("iota_e", [P, EXPERTS])
        minus_half = sb("minus_half", [P, 1])
        eps = sb("eps", [P, 1])
        waited = sb("waited", [P, 1])
        euler = sb("euler", [P, 3 * TOP_K])
        ident_b = sb("ident_b", [P, P], BF16)
        mask_bias = sb("mask_bias", [P, T, KEYS], BF16)
        ctx_dup = sb("ctx_dup", [P, C, BATCH, 2, KEYS])
        kt = sb("kt", [P, C, BATCH * KEYS])
        kt_h = sb("kt_h", [P, C, BATCH * KEYS])
        kt_l = sb("kt_l", [P, C, BATCH * KEYS])
        kbd_h = sb("kbd_h", [P, C, BATCH, HPC, KEYS], F32R)
        kbd_l = sb("kbd_l", [P, C, BATCH, HPC, KEYS], F32R)
        v_ext = sb("v_ext", [P, BATCH, HP, 2 * VW])
        wo_h = sb("wo_h", [P, C, D], F32R)
        wo_l = sb("wo_l", [P, C, D], F32R)
        g_h = sb("g_h", [P, C, ROUTES], F32R)
        g_l = sb("g_l", [P, C, ROUTES], F32R)
        w_h = sb("w_h", [P, CHUNKS, C, 2 * D], F32R)
        w_l = sb("w_l", [P, CHUNKS, C, 2 * D], F32R)
        bn = sb("bn", [P, 6])
        mean_var = sb("mean_var", [P, 2])
        var_eps = sb("var_eps", [P, 1])
        rstd = sb("rstd", [P, 1])
        xn = sb("xn", [P, D])
        xn_t = sb("xn_t", [P, C, P])
        q_h = sb("q_h", [P, C, P], F32R)
        q_l = sb("q_l", [P, C, P], F32R)
        s_d = sb("s_d", [P, HEADS, KEYS])
        s_max = sb("s_max", [P, HEADS])
        prob = sb("prob", [P, HEADS, KEYS])
        prob_t = sb("prob_t", [P, HP, P])
        r_sum = sb("r_sum", [P, HEADS])
        a_n = sb("a_n", [P, D])
        a_h = sb("a_h", [P, C, P], F32R)
        a_l = sb("a_l", [P, C, P], F32R)
        xf = sb("xf", [P, D])
        xf_h = sb("xf_h", [P, C, P], F32R)
        xf_l = sb("xf_l", [P, C, P], F32R)
        z_sb = sb("z_sb", [P, 3, EXPERTS])
        top = sb("top", [P, 3, 8])
        top_i = sb("top_i", [P, 3, 8], U32)
        top_d = sb("top_d", [P, 3, TOP_K])
        top_e = sb("top_e", [P, 3 * TOP_K])
        e_sum = sb("e_sum", [P, 3])
        e_rec = sb("e_rec", [P, 3])
        top_w = sb("top_w", [P, 3, TOP_K])
        at_e = sb("at_e", [P, 3, EXPERTS, TOP_K])
        w_at_e = sb("w_at_e", [P, 3, EXPERTS, TOP_K])
        c_new = sb("c_new", [P, 3, EXPERTS])
        c_cur = sb("c_cur", [P, 3, EXPERTS])
        c3_t = sb("c3_t", [EXPERTS, P])
        sum1 = [sb(f"sum1_{i}", [P, D]) for i in range(2)]
        sum2 = [sb(f"sum2_{i}", [P, D]) for i in range(2)]
        h_in = sb("h_in", [P, D])
        h = sb("h", [P, D])
        h_h = sb("h_h", [P, C, P], F32R)
        h_l = sb("h_l", [P, C, P], F32R)

        banks = ctx.enter_context(nc.psum_tensor("banks", [P, 8, 512], F32))
        ps_s = banks[:, 0:2, :].rearrange("p b (h k) -> p (b h) k", k=KEYS)
        ps_pt = banks[:, 2:4, :].rearrange("p b n -> p (b n)").rearrange("p (j t) -> p j t", t=P)
        ps_v = banks[:, 4, 0:HP * 2 * VW]
        ps_x = banks[:, 5, 0:D].rearrange("p (c t) -> p c t", c=C)
        ps_a = banks[:, 6, 0:D].rearrange("p (c t) -> p c t", c=C)
        ps_o = banks[:, 6, 0:D]
        ps_q = banks[:, 7, 0:D].rearrange("p (c t) -> p c t", c=C)
        ps_o_last = banks[:, 7, P:P + D]
        ps_g = banks[:, 6, 0:C * ROUTES].rearrange("p (c r) -> p c r", c=C)
        ps_t = banks[:, 5, 0:D].rearrange("p (c t) -> p c t", c=C)
        ps_c3 = banks[0:EXPERTS, 7, 0:P]
        ps_y = banks[:, 7, P:P + D]
        ps_z = banks[:, 7, P + D:P + D + ROUTES]

        x_in = [sem(f"x_in{b}") for b in range(BATCH)]
        k_in, q_in, mask_in, v_in, o_in, ffn_in = (sem(n) for n in ("k_in", "q_in", "mask_in", "v_in", "o_in", "ffn_in"))
        w_in = [sem(f"w_in{r}") for r in range(RING)]
        bv_in, bo_in = sem("bv_in"), sem("bo_in")
        consts_set = sem("consts_set")
        setup_dve = sem("setup_dve")
        kt_done, v_done, g_done = sem("kt_done"), sem("v_done"), sem("g_done")
        w_hi = sem("w_hi")
        w_split = sem("w_split")
        var_ready, rstd_ready = sem("var_ready"), sem("rstd_ready")
        xb_ready = sem("xb_ready")
        bn_done, stats_ready, xn_ready = sem("bn_done"), sem("stats_ready"), sem("xn_ready")
        xt_done, xt_copied = sem("xt_done"), sem("xt_copied")
        q_done, q_hi, q_ready = sem("q_done"), sem("q_hi"), sem("q_ready")
        s_done, s_maxed, s_ready = sem("s_done"), sem("s_maxed"), sem("s_ready")
        p_ready, pt_done, pt_copied = sem("p_ready"), sem("pt_done"), sem("pt_copied")
        pv_done, sum_rec, a_ready = sem("pv_done"), sem("sum_rec"), sem("a_ready")
        at_done, a_hi, a_lo = sem("at_done"), sem("a_hi"), sem("a_lo")
        o_done, x2_ready = sem("o_done"), sem("x2_ready")
        bn2_done, stats2_ready, xf_ready = sem("bn2_done"), sem("stats2_ready"), sem("xf_ready")
        var2_ready, rstd2_ready = sem("var2_ready"), sem("rstd2_ready")
        xft_done, xf_hi, xf_lo = sem("xft_done"), sem("xf_hi"), sem("xf_lo")
        z_done, route, e_ready = sem("z_done"), sem("route"), sem("e_ready")
        c_moved = sem("c_moved")
        c3t_done, c3t_copied, y_done = sem("c3t_done"), sem("c3t_copied"), sem("y_done")
        y_added = sem("y_added")
        pair_done = sem("pair_done")
        acc = sem("acc")
        h_ready, ht_done, h_hi, h_lo = sem("h_ready"), sem("ht_done"), sem("h_hi"), sem("h_lo")
        stored = sem("stored")

        x_dram = x.rearrange("b (p j) d -> b p j d", j=TPB)
        out_dram = out.rearrange("b (p j) d -> p b j d", j=TPB)
        mask_dram = mask.rearrange("b (p j) k -> b p j k", j=TPB)
        rows = lambda w: w.rearrange("(c p) n -> p c n", c=C)
        w_dram = [w.rearrange("(c p) e o -> p c (e o)", c=C) for w in (w1_t, w2_t)]

        block = ctx.enter_context(nc.Block())

        @block.sync
        def _(sp):
            sp.dma_start(x_all[:, 0:TPB, :], x_dram[0]).then_inc(x_in[0], 16)
            sp.dma_start(ctx_sb[:, :, :], rows(ctx_t)).then_inc(k_in, 16)
            sp.dma_start(wk_sb[:, :, :], rows(wk_t)).then_inc(k_in, 16)
            sp.dma_start(bk_sb[:, :], bk).then_inc(k_in, 16)
            sp.dma_start(wq_sb[:, :, :], rows(wq_t)).then_inc(q_in, 16)
            sp.dma_start(bq_sb[:, :], bq).then_inc(q_in, 16)
            sp.dma_start(x_all[:, TPB:T, :], x_dram[1]).then_inc(x_in[1], 16)
            for b in range(BATCH):
                sp.dma_start(mask_all[:, b * TPB:(b + 1) * TPB, :], mask_dram[b]).then_inc(mask_in, 16)
            sp.dma_start(wv_sb[:, :, :], rows(wv_t)).then_inc(v_in, 16)
            sp.dma_start(bv_sb[:, :], bv.partition_broadcast(P)).then_inc(bv_in, 16)
            sp.dma_start(bo_sb[:, :], bo.partition_broadcast(P)).then_inc(bo_in, 16)
            sp.dma_start(wo_sb[:, :, :], rows(wo_t)).then_inc(o_in, 16)
            sp.dma_start(pw_sb[:, :], p_w).then_inc(ffn_in, 16)
            sp.dma_start(u_sb[:, :], u_t).then_inc(ffn_in, 16)
            sp.dma_start(b2_sb[:, :], b2).then_inc(ffn_in, 16)
            for n in range(CHUNKS):
                layer, pair = n // PAIRS, n % PAIRS
                if n >= RING:
                    sp.wait_ge(w_split, n - RING + 1)
                sp.dma_start(stage[:, n % RING, :, :],
                             w_dram[layer][:, :, pair * 2 * D:(pair + 1) * 2 * D]).then_inc(w_in[n % RING], 16)

            def store(b, j, sums):
                sp.wait_ge(acc, sums)
                sp.dma_start(out_dram[:, b, j, :], x_all[:, j + b * TPB, :]).then_inc(stored, 16)

            for b in range(BATCH):
                with sp.Fori(0, TPB if b < BATCH - 1 else TPB - 1) as j:
                    store(b, j, 2 * SUMS * j + (2 * SUMS * b * TPB + 3 * SUMS))
            store(BATCH - 1, TPB - 1, 2 * SUMS * T)
            sp.wait_ge(stored, 16 * T)

        @block.gpsimd
        def _(pool):
            pool.memset(ident[:, :], 0.0).then_inc(consts_set, 1)
            pool.memset(ones[:, :], 1.0).then_inc(consts_set, 1)
            pool.memset(head_of[:, :], 1.0).then_inc(consts_set, 1)
            pool.memset(minus_half[:, :], -0.5).then_inc(consts_set, 1)
            pool.memset(eps[:, :], LN_EPS).then_inc(consts_set, 1)
            pool.memset(euler[:, :], EULER).then_inc(consts_set, 1)
            pool.iota(iota_e[:, :], pattern=[[1, EXPERTS]], base=0, channel_multiplier=0,
                      allow_small_or_imprecise_dtypes=True).then_inc(consts_set, 1)
            pool.wait_ge(consts_set, 7)
            pool.affine_select(out=ident[:, :], in_=ident[:, :], compare_op=ALU.not_equal, fill=1.0, base=0,
                               pattern=[[-1, P]], channel_multiplier=1).then_inc(consts_set, 1)
            pool.affine_select(out=head_of[:, :], in_=head_of[:, :], compare_op=ALU.is_ge, fill=0.0, base=0,
                               pattern=[[-DK, HPC]], channel_multiplier=1).then_inc(consts_set, 1)
            pool.wait_ge(consts_set, 9)
            pool.affine_select(out=head_of[:, :], in_=head_of[:, :], compare_op=ALU.is_ge, fill=0.0, base=DK - 1,
                               pattern=[[DK, HPC]], channel_multiplier=-1).then_inc(consts_set, 1)

            def inverse_deviation(t, stats, var, out_sem):
                pool.wait_ge(stats, t + 1)
                pool.tensor_tensor(var_eps[:, :], mean_var[:, 1:2], eps[:, :], ALU.add).then_inc(var, 1)
                pool.wait_ge(var, t + 1)
                pool.tensor_tensor(rstd[:, :], var_eps[:, :], minus_half[:, :], ALU.pow).then_inc(out_sem, 1)

            def add_output_bias(t):
                pool.wait_ge(xn_ready, t + 1)
                pool.tensor_tensor(x_all[:, t, :], x_all[:, t, :], bo_sb[:, :], ALU.add).then_inc(xb_ready, 1)

            def split_weights(n, slot):
                pool.wait_ge(w_hi, n + 1)
                pool.tensor_tensor(w_l[:, n, :, :], stage[:, slot, :, :], w_h[:, n, :, :].bitcast(F32),
                                   ALU.subtract).then_inc(w_split, 1)

            def attention(t):
                inverse_deviation(t, stats_ready, var_ready, rstd_ready)
                add_output_bias(t - 1)

            inverse_deviation(0, stats_ready, var_ready, rstd_ready)
            pool.wait_ge(bo_in, 16)
            for t in range(1, 5):
                attention(t)
            with pool.Fori(0, CHUNKS // RING - 1) as g:
                for r in range(RING):
                    attention(g * RING + (r + 5))
                    split_weights(g * RING + r, r)
            for n in range(CHUNKS - RING, CHUNKS):
                if n < CHUNKS - 1:
                    attention(n + 5)
                else:
                    add_output_bias(T - 1)
                    inverse_deviation(0, stats2_ready, var2_ready, rstd2_ready)
                split_weights(n, n % RING)

            def exponentials(t):
                pool.wait_ge(route, ROUTE_STEPS * t + ROUTE_EXP)
                pool.tensor_tensor(top_e[:, :], euler[:, :], top_d[:, :, :].rearrange("p r k -> p (r k)"),
                                   ALU.pow).then_inc(e_ready, 1)

            exponentials(0)
            with pool.Fori(1, T) as t:
                inverse_deviation(t, stats2_ready, var2_ready, rstd2_ready)
                exponentials(t)


        @block.scalar
        def _(act):
            def copy_xt(t):
                act.wait_ge(xt_done, t + 1)
                if later(t, 1):
                    act.wait_ge(q_done, t)
                nc.scalar.activation(xn_t[:, :, :], ps_x, ACT.Copy).then_inc(xt_copied, 1)

            def q_high(t):
                act.wait_ge(q_done, t + 1)
                if later(t, 1):
                    act.wait_ge(s_done, t)
                for c in range(C):
                    nc.scalar.activation(q_h[:, c, :], ps_q[:, c, :], ACT.Identity,
                                         bias=bq_sb[:, c:c + 1]).then_inc(q_hi, 1)

            def exp_scores(t):
                act.wait_ge(s_ready, t + 1)
                if later(t, 1):
                    act.wait_ge(pt_done, 2 * t)
                nc.scalar.activation(prob[:, :, :], s_d[:, :, :], ACT.Exp).then_inc(p_ready, 1)

            def copy_pt(t):
                if later(t, 1):
                    act.wait_ge(pv_done, t)
                for half in range(2):
                    act.wait_ge(pt_done, 2 * t + half + 1)
                    j = half * HP // 2
                    nc.scalar.activation(prob_t[:, j:j + HP // 2, :], ps_pt[:, j:j + HP // 2, :],
                                         ACT.Copy).then_inc(pt_copied, 1)

            def a_high(t):
                act.wait_ge(at_done, t + 1)
                if later(t, 1):
                    act.wait_ge(o_done, t)
                nc.scalar.activation(a_h[:, :, :], ps_a, ACT.Copy).then_inc(a_hi, 1)

            def xf_high(t):
                act.wait_ge(xft_done, t + 1)
                nc.scalar.activation(xf_h[:, :, :], ps_t, ACT.Copy).then_inc(xf_hi, 1)

            act.wait_ge(q_in, 32)
            copy_xt(0)
            q_high(0)
            copy_xt(1)
            q_high(1)
            exp_scores(0)
            copy_xt(2)

            copy_pt(0)
            q_high(2)
            exp_scores(1)
            copy_xt(3)

            def attention(t):
                copy_pt(t)
                a_high(t - 1)
                q_high(t + 2)
                exp_scores(t + 1)

            def split_weights(g, r):
                act.wait_ge(w_in[r], g * 16 + 16)
                nc.scalar.activation(w_h[:, g * RING + r, :, :], stage[:, r, :, :], ACT.Copy).then_inc(w_hi, 1)

            attention(1)
            copy_xt(4)
            with act.Fori(0, CHUNKS // RING - 1) as g:
                for r in range(RING):
                    attention(g * RING + (r + 2))
                    split_weights(g, r)
                    copy_xt(g * RING + (r + 5))
            for r in range(RING):
                attention(T - 2 - RING + r)
                split_weights(CHUNKS // RING - 1, r)
                if r < RING - 1:
                    copy_xt(T + 1 - RING + r)
            xf_high(0)
            copy_pt(T - 2)
            a_high(T - 3)
            exp_scores(T - 1)
            copy_pt(T - 1)
            a_high(T - 2)
            a_high(T - 1)
            xf_high(1)

            def h_high(t):
                act.wait_ge(ht_done, t + 1)
                nc.scalar.activation(h_h[:, :, :], ps_t, ACT.Copy).then_inc(h_hi, 1)

            def copy_c3t(t):
                act.wait_ge(c3t_done, t + 1)
                nc.scalar.activation(c3_t[:, :], ps_c3, ACT.Copy).then_inc(c3t_copied, 1)

            def gelu(t, acc_count):
                act.wait_ge(acc, acc_count)
                if later(t, 1):
                    act.wait_ge(ht_done, t)
                nc.scalar.activation(h[:, :], h_in[:, :], ACT.Gelu).then_inc(h_ready, 1)

            gelu(0, SUMS)

            def experts(t):
                h_high(t)
                copy_c3t(t)
                gelu(t + 1, SUMS * 2 * (t + 1))
                xf_high(t + 2)

            experts(0)
            with act.Fori(1, T - 2) as t:
                experts(t)
            h_high(T - 2)
            copy_c3t(T - 2)
            gelu(T - 1, SUMS * 2 * (T - 1))
            h_high(T - 1)
            copy_c3t(T - 1)

        @block.vector
        def _(dve):
            def statistics(t, src, done, ready):
                dve.bn_stats(bn[:, :], src[:, t, :]).then_inc(done, 1)
                dve.wait_ge(done, t + 1)
                dve.memset(waited[:, :], 0.0)
                dve.bn_aggr(mean_var[:, :], bn[:, :]).then_inc(ready, 1)

            def normalise(t, src, dst, rstd_sem, ready):
                dve.wait_ge(rstd_sem, t + 1)
                dve.tensor_scalar(dst[:, :], src[:, t, :], mean_var[:, 0:1], rstd[:, 0:1],
                                  ALU.subtract, ALU.mult).then_inc(ready, 1)

            def stats1(t):
                statistics(t, x_all, bn_done, stats_ready)

            def normalise1(t):
                if later(t, 1):
                    dve.wait_ge(xt_done, t)
                normalise(t, x_all, xn, rstd_ready, xn_ready)

            def normalise2(t):
                dve.wait_ge(xft_done, t)
                normalise(t, x_all, xf, rstd2_ready, xf_ready)

            def q_low(t):
                dve.wait_ge(q_hi, C * t + C)
                if later(t, 1):
                    dve.wait_ge(s_done, t)
                for c in range(C):
                    ins = dve.scalar_tensor_tensor(out=q_l[:, c, :], in0=ps_q[:, c, :], scalar=bq_sb[:, c:c + 1],
                                                   in1=q_h[:, c, :].bitcast(F32), op0=ALU.add, op1=ALU.subtract)
                ins.then_inc(q_ready, 1)

            def max_scores(t):
                dve.wait_ge(s_done, t + 1)
                dve.tensor_reduce(s_max[:, :], ps_s, AX_X, ALU.max).then_inc(s_maxed, 1)

            def subtract_max(t):
                if later(t, 1):
                    dve.wait_ge(p_ready, t)
                dve.wait_ge(s_maxed, t + 1)
                dve.tensor_tensor(s_d[:, :, :], ps_s, s_max[:, :].unsqueeze(2).to_broadcast([P, HEADS, KEYS]),
                                  ALU.subtract).then_inc(s_ready, 1)

            def divide_by_sum(t):
                dve.wait_ge(pv_done, t + 1)
                pv = ps_v.rearrange("p (h v) -> p h v", v=VW)
                dve.reciprocal(r_sum[:, :], pv[:, :, DK]).then_inc(sum_rec, 1)
                dve.wait_ge(sum_rec, t + 1)
                if later(t, 1):
                    dve.wait_ge(at_done, t)
                dve.tensor_tensor(a_n[:, :].rearrange("p (h v) -> p h v", v=DK), pv[:, :, 0:DK],
                                  r_sum[:, :].unsqueeze(2).to_broadcast([P, HEADS, DK]),
                                  ALU.mult).then_inc(a_ready, 1)

            def a_low(t):
                dve.wait_ge(a_hi, t + 1)
                if later(t, 1):
                    dve.wait_ge(o_done, t)
                dve.tensor_tensor(a_l[:, :, :], ps_a, a_h[:, :, :].bitcast(F32), ALU.subtract).then_inc(a_lo, 1)

            def add_attention(t):
                dve.wait_ge(o_done, t + 1)
                dve.wait_ge(xb_ready, t + 1)
                o = ps_o_last if isinstance(t, int) and t == T - 1 else ps_o
                dve.tensor_tensor(x_all[:, t, :], o, x_all[:, t, :], ALU.add).then_inc(x2_ready, 1)

            dve.wait_ge(x_in[0], 16)
            stats1(0)
            normalise1(0)
            stats1(1)
            dve.wait_ge(k_in, 48)
            dve.tensor_copy(ctx_dup[:, :, :, :, :],
                            ctx_sb[:, :, :].rearrange("p c (b k) -> p (c b) k", b=BATCH).unsqueeze(2)
                            .to_broadcast([P, C * BATCH, 2, KEYS])).then_inc(setup_dve, 1)
            dve.wait_ge(kt_done, 1)
            for c in range(C):
                dve.tensor_scalar(kt[:, c, :], banks[:, 0, c * P:(c + 1) * P], bk_sb[:, c:c + 1], SCALE,
                                  ALU.add, ALU.mult).then_inc(setup_dve, 1)
            dve.wait_ge(setup_dve, 3)
            dve.tensor_copy(kt_h[:, :, :].bitcast(F32R), kt[:, :, :]).then_inc(setup_dve, 1)
            dve.wait_ge(setup_dve, 4)
            dve.tensor_tensor(kt_l[:, :, :], kt[:, :, :], kt_h[:, :, :], ALU.subtract).then_inc(setup_dve, 1)
            dve.wait_ge(setup_dve, 5)
            dve.wait_ge(consts_set, 10)
            for b in range(BATCH):
                for c in range(C):
                    for dst, src in ((kbd_h, kt_h), (kbd_l, kt_l)):
                        dve.tensor_tensor(dst[:, c, b, :, :],
                                          src[:, c, b * KEYS:(b + 1) * KEYS].unsqueeze(1).to_broadcast([P, HPC, KEYS]),
                                          head_of[:, :].unsqueeze(2).to_broadcast([P, HPC, KEYS]),
                                          ALU.mult).then_inc(setup_dve, 1)
            dve.wait_ge(mask_in, 32)
            dve.tensor_scalar(mask_bias[:, :, :], mask_all[:, :, :], 0, MASKED, ALU.is_equal,
                              ALU.mult).then_inc(setup_dve, 1)
            dve.tensor_copy(ident_b[:, :], ident[:, :]).then_inc(setup_dve, 1)
            q_low(0)
            normalise1(1)
            stats1(2)
            dve.memset(v_ext[:, :, :, :], 0.0).then_inc(setup_dve, 1)
            dve.wait_ge(setup_dve, KBD + 3)
            dve.wait_ge(bv_in, 16)
            dve.wait_ge(v_done, 1)
            for b in range(BATCH):
                for side in range(2):
                    r = slice(side * KEYS, (side + 1) * KEYS)
                    v = banks[r, 2 + b, 0:D].rearrange("p (j s v) -> p j s v", s=2, v=DK)[:, :, side, :]
                    bias = bv_sb[r, :].rearrange("p (j s v) -> p j s v", s=2, v=DK)[:, :, side, :]
                    dve.tensor_tensor(v_ext[r, b, :, side * VW:side * VW + DK], v, bias,
                                      ALU.add).then_inc(setup_dve, 1)
                    dve.memset(v_ext[r, b, :, side * VW + DK], 1.0).then_inc(setup_dve, 1)

            max_scores(0)
            subtract_max(0)
            q_low(1)
            normalise1(2)
            stats1(3)

            max_scores(1)
            subtract_max(1)
            q_low(2)
            normalise1(3)
            dve.wait_ge(o_in, 16)
            dve.tensor_copy(wo_h[:, :, :], wo_sb[:, :, :]).then_inc(setup_dve, 1)
            divide_by_sum(0)
            dve.wait_ge(setup_dve, KBD + 12)
            dve.tensor_tensor(wo_l[:, :, :], wo_sb[:, :, :], wo_h[:, :, :].bitcast(F32),
                              ALU.subtract).then_inc(setup_dve, 1)
            dve.wait_ge(g_done, 1)
            for c in range(C):
                dve.tensor_copy(g_h[:, c, :], ps_g[:, c, :]).then_inc(setup_dve, 1)
            dve.wait_ge(setup_dve, KBD + 15)
            for c in range(C):
                dve.tensor_tensor(g_l[:, c, :], ps_g[:, c, :], g_h[:, c, :].bitcast(F32),
                                  ALU.subtract).then_inc(setup_dve, 1)
            stats1(4)

            def attention(t):
                max_scores(t + 1)
                subtract_max(t + 1)
                a_low(t - 1)
                q_low(t + 2)
                normalise1(t + 3)
                divide_by_sum(t)
                add_attention(t - 1)

            attention(1)
            stats1(5)
            dve.wait_ge(x_in[1], 16)
            with dve.Fori(2, T - 4) as t:
                attention(t)
                stats1(t + 4)
            attention(T - 4)

            def xf_low(t):
                dve.wait_ge(xf_hi, t + 1)
                dve.tensor_tensor(xf_l[:, :, :], ps_t, xf_h[:, :, :].bitcast(F32), ALU.subtract).then_inc(xf_lo, 1)

            def h_low(t):
                dve.wait_ge(h_hi, t + 1)
                dve.tensor_tensor(h_l[:, :, :], ps_t, h_h[:, :, :].bitcast(F32), ALU.subtract).then_inc(h_lo, 1)

            def find_top(t):
                n = ROUTE_STEPS * t
                dve.wait_ge(z_done, t + 1)
                dve.tensor_copy(z_sb[:, :, :].rearrange("p r e -> p (r e)"), ps_z).then_inc(route, 1)
                dve.wait_ge(route, n + ROUTE_Z)
                dve.memset(waited[:, :], 0.0)
                for r in range(3):
                    dve.max(top[:, r, :], z_sb[:, r, :]).then_inc(route, 1)
                dve.wait_ge(route, n + ROUTE_TOP)
                if later(t, 1):
                    dve.wait_ge(e_ready, t)
                dve.tensor_tensor(top_d[:, :, :], top[:, :, 0:TOP_K],
                                  top[:, :, 0:1].to_broadcast([P, 3, TOP_K]), ALU.subtract).then_inc(route, 1)
                for r in range(3):
                    dve.max_index(top_i[:, r, :], top[:, r, :], z_sb[:, r, :]).then_inc(route, 1)

            def combine_weights(t):
                n = ROUTE_STEPS * t + ROUTE_INDEX
                dve.wait_ge(route, n)
                dve.tensor_tensor(at_e[:, :, :, :],
                                  top_i[:, :, 0:TOP_K].unsqueeze(2).to_broadcast([P, 3, EXPERTS, TOP_K]),
                                  iota_e[:, :].unsqueeze(1).unsqueeze(3).to_broadcast([P, 3, EXPERTS, TOP_K]),
                                  ALU.is_equal).then_inc(route, 1)
                dve.wait_ge(e_ready, t + 1)
                e = top_e[:, :].rearrange("p (r k) -> p r k", r=3)
                dve.tensor_reduce(e_sum[:, :], e, AX_X, ALU.add).then_inc(route, 1)
                dve.wait_ge(route, n + 2)
                dve.reciprocal(e_rec[:, :], e_sum[:, :]).then_inc(route, 1)
                dve.wait_ge(route, n + 3)
                dve.tensor_tensor(top_w[:, :, :], e, e_rec[:, :].unsqueeze(2).to_broadcast([P, 3, TOP_K]),
                                  ALU.mult).then_inc(route, 1)
                dve.wait_ge(route, n + 4)
                dve.tensor_tensor(w_at_e[:, :, :, :], at_e[:, :, :, :],
                                  top_w[:, :, :].unsqueeze(2).to_broadcast([P, 3, EXPERTS, TOP_K]),
                                  ALU.mult).then_inc(route, 1)
                dve.wait_ge(route, n + 5)
                if later(t, 1):
                    dve.wait_ge(c_moved, t)
                dve.tensor_reduce(c_new[:, :, :], w_at_e[:, :, :, :], AX_X, ALU.add).then_inc(route, 1)

            def move_weights(t):
                dve.wait_ge(route, ROUTE_STEPS * (t + 1))
                if later(t, 1):
                    dve.wait_ge(c3t_done, t)
                    dve.wait_ge(acc, SUMS * (2 * t + 1))
                dve.tensor_copy(c_cur[:, :, :], c_new[:, :, :]).then_inc(c_moved, 1)

            def sum_pair(slot, pair, weights, sums, added):
                dve.wait_ge(pair_done, PAIRS * slot + pair + 1)
                for e in (2 * pair, 2 * pair + 1):
                    product = banks[:, BANK[pair], (e % 2) * D:(e % 2 + 1) * D]
                    if pair == 0 and e >= added:
                        dve.tensor_scalar(sums[e % 2][:, :], product, weights[:, e:e + 1], None,
                                          ALU.mult).then_inc(acc, 1)
                        continue
                    if pair > 0:
                        dve.wait_ge(acc, SUMS * slot + e - 1)
                    dve.scalar_tensor_tensor(out=sums[e % 2][:, :], in0=product, scalar=weights[:, e:e + 1],
                                             in1=sums[e % 2][:, :], op0=ALU.mult, op1=ALU.add).then_inc(acc, 1)

            def last_sum(slot, sums, dst):
                dve.wait_ge(acc, SUMS * slot + EXPERTS)
                dve.tensor_tensor(dst, sums[0][:, :], sums[1][:, :], ALU.add).then_inc(acc, 1)

            def layer1_pairs(t, pairs):
                for pair in pairs:
                    if pair == 0:
                        dve.wait_ge(route, ROUTE_STEPS * (t + 1))
                    if pair == 0 and later(t, 1):
                        dve.wait_ge(h_ready, t)
                    sum_pair(slot1(t), pair, c_new[:, 0, :], sum1, 0)
                    if pair == PAIRS - 1:
                        last_sum(slot1(t), sum1, h_in[:, :])

            def start_layer2(t):
                dve.wait_ge(y_done, t + 1)
                dve.tensor_tensor(sum2[0][:, :], ps_y, x_all[:, t, :], ALU.add).then_inc(y_added, 1)
                dve.wait_ge(y_added, t + 1)
                dve.wait_ge(c_moved, t + 1)

            def layer2_pairs(t, pairs):
                for pair in pairs:
                    sum_pair(slot2(t), pair, c_cur[:, 1, :], sum2, 1)
                    if pair == PAIRS - 1:
                        last_sum(slot2(t), sum2, x_all[:, t, :])

            max_scores(T - 2)
            subtract_max(T - 2)
            statistics(0, x_all, bn2_done, stats2_ready)
            a_low(T - 4)
            q_low(T - 1)
            normalise(0, x_all, xf, rstd2_ready, xf_ready)
            divide_by_sum(T - 3)
            add_attention(T - 4)

            max_scores(T - 1)
            subtract_max(T - 1)
            a_low(T - 3)
            xf_low(0)
            statistics(1, x_all, bn2_done, stats2_ready)
            find_top(0)
            divide_by_sum(T - 2)
            add_attention(T - 3)
            combine_weights(0)
            normalise2(1)

            layer1_pairs(0, range(0, 2))
            a_low(T - 2)
            divide_by_sum(T - 1)
            add_attention(T - 2)
            layer1_pairs(0, range(2, 3))
            a_low(T - 1)
            layer1_pairs(0, range(3, PAIRS))
            xf_low(1)
            add_attention(T - 1)
            find_top(1)
            move_weights(0)
            combine_weights(1)

            def experts(t, ahead=True):
                if ahead:
                    statistics(t + 2, x_all, bn2_done, stats2_ready)
                layer1_pairs(t + 1, range(0, 3))
                if ahead:
                    normalise2(t + 2)
                layer1_pairs(t + 1, range(3, 4))
                h_low(t)
                layer1_pairs(t + 1, range(4, PAIRS))
                start_layer2(t)
                layer2_pairs(t, range(0, 1))
                if ahead:
                    xf_low(t + 2)
                layer2_pairs(t, range(1, 4))
                if ahead:
                    find_top(t + 2)
                layer2_pairs(t, range(4, PAIRS))
                move_weights(t + 1)
                if ahead:
                    combine_weights(t + 2)

            experts(0)
            with dve.Fori(1, T - 2) as t:
                experts(t)
            experts(T - 2, ahead=False)
            h_low(T - 1)
            start_layer2(T - 1)
            layer2_pairs(T - 1, range(PAIRS))

        @block.tensor
        def _(pe):
            def split_product(dst, left, right):
                (lh, ll), (rh, rl) = left, right
                terms = [(c, a, b) for c in range(C) for a, b in ((lh, rh), (ll, rh), (lh, rl))]
                for i, (c, a, b) in enumerate(terms):
                    ins = pe.matmul(dst, a(c), b(c), start=(i == 0), stop=(i == len(terms) - 1))
                return ins

            def whole(w):
                return lambda c: w[:, c, :]

            def keys_project():
                pe.wait_ge(k_in, 48)
                for m in range(C):
                    for c in range(C):
                        ins = pe.matmul(banks[:, 0, m * P:(m + 1) * P], wk_sb[:, c, m * P:(m + 1) * P],
                                        ctx_sb[:, c, :], start=(c == 0), stop=(c == C - 1))
                ins.then_inc(kt_done, 1)

            def values_project():
                pe.wait_ge(v_in, 16)
                pe.wait_ge(setup_dve, 1)
                for b in range(BATCH):
                    for c in range(C):
                        ins = pe.matmul(banks[:, 2 + b, 0:D], ctx_dup[:, c, b, :, :].rearrange("p s k -> p (s k)"),
                                        wv_sb[:, c, :], start=(c == 0), stop=(c == C - 1))
                ins.then_inc(v_done, 1)

            def router_weights():
                pe.wait_ge(ffn_in, 48)
                for c in range(C):
                    ins = pe.matmul(ps_g[:, c, :], pw_sb[:, c * P:(c + 1) * P],
                                    u_sb[:, :], start=True, stop=True)
                ins.then_inc(g_done, 1)

            def transpose_x(t):
                pe.wait_ge(xn_ready, t + 1)
                if later(t, 1):
                    pe.wait_ge(xt_copied, t)
                for c in range(C):
                    ins = pe.transpose(ps_x[:, c, :], xn[:, c * P:(c + 1) * P], ident[:, :])
                ins.then_inc(xt_done, 1)

            def queries(t):
                pe.wait_ge(xt_copied, t + 1)
                if later(t, 1):
                    pe.wait_ge(q_ready, t)
                for m in range(C):
                    for c in range(C):
                        ins = pe.matmul(ps_q[:, m, :], wq_sb[:, c, m * P:(m + 1) * P], xn_t[:, c, :],
                                        start=(c == 0), stop=(c == C - 1))
                ins.then_inc(q_done, 1)

            def scores(t, b):
                pe.wait_ge(q_ready, t + 1)
                if later(t, 1):
                    pe.wait_ge(s_ready, t)
                for c in range(C):
                    kh = kbd_h[:, c, b, :, :].rearrange("p h k -> p (h k)")
                    kl = kbd_l[:, c, b, :, :].rearrange("p h k -> p (h k)")
                    pe.matmul(banks[:, c, :].rearrange("p (h k) -> p h k", k=KEYS), ident_b[:, :],
                              mask_bias[:, t, :].unsqueeze(1).to_broadcast([P, HPC, KEYS]), start=True, stop=False)
                    pe.matmul(banks[:, c, :], q_h[:, c, :], kh, start=False, stop=False)
                    pe.matmul(banks[:, c, :], q_l[:, c, :], kh, start=False, stop=False)
                    ins = pe.matmul(banks[:, c, :], q_h[:, c, :], kl, start=False, stop=True)
                ins.then_inc(s_done, 1)

            def transpose_probs(t):
                pe.wait_ge(p_ready, t + 1)
                if later(t, 1):
                    pe.wait_ge(pt_copied, 2 * t)
                for half in range(2):
                    for j in range(half * HP // 2, (half + 1) * HP // 2):
                        ins = pe.transpose(ps_pt[:, j, :], prob[:, 2 * j:2 * j + 2, :].rearrange("p h k -> p (h k)"),
                                           ident[:, :])
                    ins.then_inc(pt_done, 1)

            def weigh_values(t, b):
                if later(t, 1):
                    pe.wait_ge(a_ready, t)
                for half in range(2):
                    pe.wait_ge(pt_copied, 2 * t + half + 1)
                    for j in range(half * HP // 2, (half + 1) * HP // 2):
                        ins = pe.matmul(ps_v[:, j * 2 * VW:(j + 1) * 2 * VW], prob_t[:, j, :], v_ext[:, b, j, :],
                                        start=True, stop=True)
                ins.then_inc(pv_done, 1)

            def transpose_a(t):
                pe.wait_ge(a_ready, t + 1)
                if later(t, 1):
                    pe.wait_ge(x2_ready, t)
                for c in range(C):
                    ins = pe.transpose(ps_a[:, c, :], a_n[:, c * P:(c + 1) * P], ident[:, :])
                ins.then_inc(at_done, 1)

            def output_project(t):
                pe.wait_ge(a_lo, t + 1)
                o = ps_o_last if isinstance(t, int) and t == T - 1 else ps_o
                split_product(o, (whole(a_h), whole(a_l)), (whole(wo_h), whole(wo_l))).then_inc(o_done, 1)

            def transpose_xf(t):
                pe.wait_ge(xf_ready, t + 1)
                if later(t, 2):
                    pe.wait_ge(h_lo, t - 1)
                else:
                    pe.wait_ge(xf_lo if t else xt_copied, 1 if t else T)
                for c in range(C):
                    ins = pe.transpose(ps_t[:, c, :], xf[:, c * P:(c + 1) * P], ident[:, :])
                ins.then_inc(xft_done, 1)

            def logits(t):
                pe.wait_ge(xf_lo, t + 1)
                if later(t, 2):
                    pe.wait_ge(y_added, t - 1)
                elif t == 1:
                    pe.wait_ge(x2_ready, T)
                split_product(ps_z, (whole(xf_h), whole(xf_l)), (whole(g_h), whole(g_l))).then_inc(z_done, 1)

            def transpose_h(t):
                pe.wait_ge(h_ready, t + 1)
                pe.wait_ge(xf_lo, min(t + 2, T) if isinstance(t, int) else t + 2)
                for c in range(C):
                    ins = pe.transpose(ps_t[:, c, :], h[:, c * P:(c + 1) * P], ident[:, :])
                ins.then_inc(ht_done, 1)

            def transpose_c3(t):
                pe.wait_ge(c_moved, t + 1)
                if later(t, 1):
                    pe.wait_ge(y_added, t)
                pe.transpose(ps_c3, c_cur[:, 2, :], ident[:, :]).then_inc(c3t_done, 1)

            def expert_bias(t):
                pe.wait_ge(c3t_copied, t + 1)
                pe.matmul(ps_y, c3_t[:, :], b2_sb[:, :], start=True, stop=True).then_inc(y_done, 1)

            def expert_pairs(slot, pairs, left, layer):
                for pair in pairs:
                    if later(slot, 1):
                        pe.wait_ge(acc, SUMS * slot - SUMS + 2 * pair + 2)
                    n = layer * PAIRS + pair
                    split_product(banks[:, BANK[pair], :], left,
                                  (lambda c: w_h[:, n, c, :], lambda c: w_l[:, n, c, :])).then_inc(pair_done, 1)

            xf_parts, h_parts = (whole(xf_h), whole(xf_l)), (whole(h_h), whole(h_l))

            pe.wait_ge(consts_set, 10)
            transpose_x(0)
            keys_project()
            pe.wait_ge(q_in, 32)
            queries(0)
            transpose_x(1)
            values_project()
            pe.wait_ge(setup_dve, KBD + 2)
            scores(0, 0)
            queries(1)
            router_weights()
            transpose_x(2)

            scores(1, 0)
            pe.wait_ge(setup_dve, KBD + 3 + 4 * BATCH)
            transpose_probs(0)
            queries(2)
            weigh_values(0, 0)
            transpose_x(3)
            pe.wait_ge(setup_dve, SETUP)

            def attention(t, b, b_next):
                scores(t + 1, b_next)
                transpose_probs(t)
                transpose_a(t - 1)
                queries(t + 2)
                weigh_values(t, b)
                output_project(t - 1)

            attention(1, 0, 0)
            transpose_x(4)
            with pe.Fori(2, T - 3) as t:
                attention(t, t // TPB, (t + 1) // TPB)
                transpose_x(t + 3)

            attention(T - 3, BATCH - 1, BATCH - 1)
            transpose_xf(0)

            scores(T - 1, BATCH - 1)
            transpose_probs(T - 2)
            transpose_a(T - 3)
            logits(0)
            weigh_values(T - 2, BATCH - 1)
            output_project(T - 3)

            pe.wait_ge(w_split, PAIRS)
            pe.wait_ge(s_ready, T)
            expert_pairs(0, range(0, 2), xf_parts, 0)
            transpose_probs(T - 1)
            transpose_a(T - 2)
            weigh_values(T - 1, BATCH - 1)
            output_project(T - 2)
            expert_pairs(0, range(2, 4), xf_parts, 0)
            transpose_a(T - 1)
            expert_pairs(0, range(4, 5), xf_parts, 0)
            pe.wait_ge(a_lo, T)
            expert_pairs(0, range(5, PAIRS), xf_parts, 0)
            transpose_xf(1)
            output_project(T - 1)
            logits(1)
            pe.wait_ge(w_split, CHUNKS)

            def experts(t, ahead=True):
                expert_pairs(slot1(t + 1), range(0, 3), xf_parts, 0)
                transpose_h(t)
                transpose_c3(t)
                expert_pairs(slot1(t + 1), range(3, PAIRS), xf_parts, 0)
                expert_bias(t)
                pe.wait_ge(h_lo, t + 1)
                if ahead:
                    transpose_xf(t + 2)
                expert_pairs(slot2(t), range(0, 3), h_parts, 1)
                if ahead:
                    logits(t + 2)
                expert_pairs(slot2(t), range(3, PAIRS), h_parts, 1)

            experts(0)
            with pe.Fori(1, T - 2) as t:
                experts(t)
            experts(T - 2, ahead=False)
            transpose_h(T - 1)
            transpose_c3(T - 1)
            expert_bias(T - 1)
            pe.wait_ge(h_lo, T)
            expert_pairs(2 * T - 1, range(PAIRS), h_parts, 1)


_INS = ["x", "mask", "ctx_t", "wq_t", "bq", "wk_t", "bk", "wv_t", "bv", "wo_t", "bo", "p_w", "u_t", "w1_t", "w2_t", "b2"]
_OUTS = [((2, 1024, 256), "float32")]


def kernel(x, ctx_1024, mask_BxSxS2_ik1, L0_xattn_Wq, L0_xattn_bq, L0_xattn_Wk, L0_xattn_bk, L0_xattn_Wv,
           L0_xattn_bv, L0_xattn_Wo, L0_xattn_bo, L0_ffn_P_w, L0_ffn_U1, L0_ffn_U2, L0_ffn_U3, L0_ffn_W1,
           L0_ffn_W2, L0_ffn_b2):
    import numpy as _np
    import concourse.bacc as _bacc
    from concourse import mybir as _mybir
    from concourse.bass_utils import run_bass_kernel_spmd as _run

    d = x.shape[-1]
    columns = lambda v: _np.asarray(v).reshape(-1, P).T
    laid_out = {
        "x": x, "mask": mask_BxSxS2_ik1,
        "ctx_t": _np.asarray(ctx_1024).reshape(-1, d).T,
        "wq_t": _np.asarray(L0_xattn_Wq).T, "bq": columns(L0_xattn_bq),
        "wk_t": _np.asarray(L0_xattn_Wk).T, "bk": columns(L0_xattn_bk),
        "wv_t": _np.asarray(L0_xattn_Wv).T, "bv": _np.asarray(L0_xattn_bv),
        "wo_t": _np.asarray(L0_xattn_Wo).T, "bo": _np.asarray(L0_xattn_bo),
        "p_w": L0_ffn_P_w,
        "u_t": _np.concatenate([_np.asarray(u) for u in (L0_ffn_U1, L0_ffn_U2, L0_ffn_U3)], axis=0).T,
        "w1_t": _np.asarray(L0_ffn_W1).transpose(2, 0, 1), "w2_t": _np.asarray(L0_ffn_W2).transpose(2, 0, 1),
        "b2": L0_ffn_b2,
    }
    nc = _bacc.Bacc("TRN2", target_bir_lowering=False, num_devices=1)
    arrays, args = {}, []
    for name in _INS:
        a = _np.ascontiguousarray(laid_out[name])
        arrays[f"in_{name}_dram"] = a
        args.append(nc.dram_tensor(f"in_{name}_dram", a.shape, _mybir.dt.from_np(a.dtype), kind="ExternalInput").ap())
    for i, (shape, dtype) in enumerate(_OUTS):
        dt = _mybir.dt.from_np(_np.dtype(dtype))
        args.append(nc.dram_tensor(f"out_{i}_dram", shape, dt, kind="ExternalOutput").ap())
    xattn_ffn_kernel(nc, *args)
    r = _run(nc, [arrays], core_ids=[0])
    return r.results[0]["out_0_dram"]
```

```python
from contextlib import ExitStack

import concourse.bass as bass
from concourse import mybir

ALU = mybir.AluOpType
ACT = mybir.ActivationFunctionType
AX_X = mybir.AxisListType.X
F32 = mybir.dt.float32
F32R = mybir.dt.float32r
BF16 = mybir.dt.bfloat16
I32 = mybir.dt.int32
U32 = mybir.dt.uint32

P = 128
MASKED = -2.0 ** 99
LN_EPS = 1e-5
EULER = 2.718281828459045
TOP_K = 3


def xattn_ffn_kernel(nc: bass.Bass, x, mask, ctx_t, wq_t, bq, wk_t, bk, wv_t, bv, wo_t, bo,
                     p_w, u_t, w1_t, w2_t, b2, out):
    BATCH, SEQ, D = x.shape
    KEYS = mask.shape[2]
    HEADS = 16
    DK = D // HEADS
    C = D // P
    TPB = SEQ // P
    T = BATCH * TPB
    EXPERTS = w1_t.shape[1]
    PAIRS = EXPERTS // 2
    ROUTES = 3 * EXPERTS
    HPC = P // DK
    HP = HEADS // 2
    VW = DK + 1
    CHUNKS = 2 * PAIRS
    RING = 3
    SCALE = float(DK) ** -0.5
    assert 2 * KEYS == P and C == 2 and EXPERTS % 2 == 0 and CHUNKS == T - 4

    def later(t, n):
        return not isinstance(t, int) or t >= n

    def slot1(t):
        return 0 if isinstance(t, int) and t == 0 else 2 * t - 1

    def slot2(t):
        return 2 * T - 1 if isinstance(t, int) and t == T - 1 else 2 * t + 2

    HPG = HPC // 2
    HALF = P // 2
    KBD = 7
    V_SET = KBD + 2 * BATCH
    SETUP = V_SET + 2
    ROW = 32
    SUMS = EXPERTS + 1
    BANK = (0, 1, 2, 3, 4, 6)
    ROUTE_Z, ROUTE_TOP, ROUTE_EXP, ROUTE_INDEX, ROUTE_STEPS = 1, 4, 5, 8, 14

    with ExitStack() as ctx:
        def sb(name, shape, dt=F32):
            return ctx.enter_context(nc.sbuf_tensor(name, shape, dt))

        def sem(name):
            return ctx.enter_context(nc.semaphore(name))

        x_all = sb("x_all", [P, T, D])
        mask_all = sb("mask_all", [P, T, KEYS], I32)
        ctx_sb = sb("ctx_sb", [P, C, BATCH * KEYS])
        wk_sb = sb("wk_sb", [P, C, D])
        wq_sb = sb("wq_sb", [P, C, D])
        wv_sb = sb("wv_sb", [P, C, D])
        wo_sb = sb("wo_sb", [P, C, D])
        bq_sb = sb("bq_sb", [P, C])
        bk_sb = sb("bk_sb", [P, C])
        bv_sb = sb("bv_sb", [P, D])
        bo_sb = sb("bo_sb", [P, D])
        pw_sb = sb("pw_sb", [p_w.shape[0], D])
        u_sb = sb("u_sb", [p_w.shape[0], ROUTES])
        b2_sb = sb("b2_sb", [3 * ROW, D])
        stage = sb("stage", [P, RING, C, 2 * D])
        ident = sb("ident", [P, P])
        ones = sb("ones", [P, P])
        head_of = sb("head_of", [P, HPC])
        head_in = sb("head_in", [P, HPG])
        iota_e = sb("iota_e", [P, EXPERTS])
        minus_half = sb("minus_half", [P, 1])
        eps = sb("eps", [P, 1])
        waited = sb("waited", [P, 1])
        euler = sb("euler", [P, 3 * TOP_K])
        ident_b = sb("ident_b", [P, P], BF16)
        mask_bias = sb("mask_bias", [P, T, KEYS], BF16)
        ctx_dup = sb("ctx_dup", [P, C, BATCH, 2, KEYS])
        kt = sb("kt", [P, C, BATCH * KEYS])
        kt_h = sb("kt_h", [P, C, BATCH * KEYS])
        kt_l = sb("kt_l", [P, C, BATCH * KEYS])
        kt_hh = sb("kt_hh", [P, C, 2, BATCH * KEYS])
        kbd_hh = sb("kbd_hh", [P, BATCH, C, 2, HPG, KEYS], F32R)
        kbd_l = sb("kbd_l", [P, BATCH, C, HPC, KEYS], F32R)
        v_ext = sb("v_ext", [P, BATCH, HP, 2 * VW])
        wo_h = sb("wo_h", [P, C, D], F32R)
        wo_l = sb("wo_l", [P, C, D], F32R)
        router_w = sb("router_w", [P, C, ROUTES])
        b2_hhl = sb("b2_hhl", [3 * ROW, D], F32R)
        w_h = sb("w_h", [P, CHUNKS, C, 2 * D], F32R)
        w_l = sb("w_l", [P, CHUNKS, C, 2 * D], F32R)
        bn = sb("bn", [P, 6])
        mean_var = sb("mean_var", [P, 2])
        var_eps = sb("var_eps", [P, 1])
        rstd = sb("rstd", [P, 1])
        xn = sb("xn", [P, D])
        xn_t = sb("xn_t", [P, C, P])
        q = sb("q", [P, C, P])
        q_hl = sb("q_hl", [P, C, 2, P], F32R)
        q_h = sb("q_h", [P, C, P], F32R)
        s_d = sb("s_d", [P, HEADS, KEYS])
        s_max = sb("s_max", [P, HEADS])
        prob = sb("prob", [P, HEADS, KEYS])
        prob_t = sb("prob_t", [P, HP, P])
        r_sum = sb("r_sum", [P, HEADS])
        a_n = sb("a_n", [P, D])
        a_h = sb("a_h", [P, C, P], F32R)
        a_l = sb("a_l", [P, C, P], F32R)
        xf = sb("xf", [P, D])
        xf_t = sb("xf_t", [P, C, P])
        xf_h = sb("xf_h", [P, C, P], F32R)
        xf_l = sb("xf_l", [P, C, P], F32R)
        z_sb = sb("z_sb", [P, 3, EXPERTS])
        top = sb("top", [P, 3, 8])
        top_i = sb("top_i", [P, 3, 8], U32)
        top_d = sb("top_d", [P, 3, TOP_K])
        top_e = sb("top_e", [P, 3 * TOP_K])
        e_sum = sb("e_sum", [P, 3])
        e_rec = sb("e_rec", [P, 3])
        top_w = sb("top_w", [P, 3, TOP_K])
        at_e = sb("at_e", [P, 3, EXPERTS, TOP_K])
        w_at_e = sb("w_at_e", [P, 3, EXPERTS, TOP_K])
        c_new = sb("c_new", [P, 3, EXPERTS])
        c_cur = sb("c_cur", [P, 3, EXPERTS])
        c3_hlh = sb("c3_hlh", [P, 3, ROW])
        c3_t = sb("c3_t", [3 * ROW, P], F32R)
        sum1 = [sb(f"sum1_{i}", [P, D]) for i in range(2)]
        sum2 = [s_d[:, :, :].rearrange("p h k -> p (h k)")[:, i * D:(i + 1) * D] for i in range(2)]
        h_in = xn
        h = xn_t[:, :, :].rearrange("p c t -> p (c t)")
        h_h = sb("h_h", [P, C, P], F32R)
        h_l = sb("h_l", [P, C, P], F32R)

        banks = ctx.enter_context(nc.psum_tensor("banks", [P, 8, 512], F32))
        ps_s = banks[:, 0:2, :].rearrange("p b (h k) -> p (b h) k", k=KEYS)
        ps_pt = banks[:, 2:4, :].rearrange("p b n -> p (b n)").rearrange("p (j t) -> p j t", t=P)
        ps_v = banks[:, 4, 0:HP * 2 * VW]
        ps_x = banks[:, 5, 0:D].rearrange("p (c t) -> p c t", c=C)
        ps_a = banks[:, 6, 0:D].rearrange("p (c t) -> p c t", c=C)
        ps_o = banks[:, 6, 0:D]
        ps_q = banks[:, 7, 0:D].rearrange("p (c t) -> p c t", c=C)
        ps_o_last = banks[:, 7, P:P + D]
        ps_g = banks[:, 6, 0:C * ROUTES].rearrange("p (c r) -> p c r", c=C)
        ps_t = banks[:, 5, 0:D].rearrange("p (c t) -> p c t", c=C)
        ps_c3 = banks[0:3 * ROW, 7, 0:P]
        ps_y = banks[:, 7, P:P + D]
        ps_z = banks[:, 7, P + D:P + D + ROUTES]

        def place_high_keys(engine, b, signal):
            engine.tensor_tensor(kbd_hh[:, b, :, :, :, :].rearrange("p c g h k -> p (c g) h k"),
                                 kt_hh[:, :, :, b * KEYS:(b + 1) * KEYS].rearrange("p c g k -> p (c g) k").unsqueeze(2)
                                 .to_broadcast([P, 2 * C, HPG, KEYS]),
                                 head_in[:, :].unsqueeze(1).unsqueeze(3).to_broadcast([P, 2 * C, HPG, KEYS]),
                                 ALU.mult).then_inc(signal, 1)

        def place_low_keys(engine, b, signal):
            engine.tensor_tensor(kbd_l[:, b, :, :, :],
                                 kt_l[:, :, b * KEYS:(b + 1) * KEYS].unsqueeze(2).to_broadcast([P, C, HPC, KEYS]),
                                 head_of[:, :].unsqueeze(1).unsqueeze(3).to_broadcast([P, C, HPC, KEYS]),
                                 ALU.mult).then_inc(signal, 1)

        def mask_keys(engine, b, signal):
            engine.wait_ge(mask_in[b], 16)
            engine.tensor_scalar(mask_bias[:, b * TPB:(b + 1) * TPB, :], mask_all[:, b * TPB:(b + 1) * TPB, :],
                                 0, MASKED, ALU.is_equal, ALU.mult).then_inc(signal, 1)

        def is_last(t):
            return isinstance(t, int) and t == T - 1

        def h_buffers(t):
            return (xf_h, xf_l) if is_last(t) else (h_h, h_l)

        def weights2(t):
            return c_new if is_last(t) else c_cur

        x_in = [sem(f"x_in{i}") for i in range(4)]
        k_in, q_in, v_in, o_in, ffn_in = (sem(n) for n in ("k_in", "q_in", "v_in", "o_in", "ffn_in"))
        mask_in = [sem(f"mask_in{b}") for b in range(BATCH)]
        ctx_in, bq_in = sem("ctx_in"), sem("bq_in")
        w_in = [sem(f"w_in{r}") for r in range(RING)]
        bv_in, bo_in = sem("bv_in"), sem("bo_in")
        consts_set = sem("consts_set")
        setup_dve = sem("setup_dve")
        kt_done, v_done, g_done = sem("kt_done"), sem("v_done"), sem("g_done")
        ident_b_set, wo_hi, b2_hi = sem("ident_b_set"), sem("wo_hi"), sem("b2_hi")
        kt_hh_set = sem("kt_hh_set")
        mask_set, kbd_set, wo_lo = sem("mask_set"), sem("kbd_set"), sem("wo_lo")
        w_hi = sem("w_hi")
        w_split = sem("w_split")
        bn_done, stats_ready = sem("bn_done"), sem("stats_ready")
        var_ready, rstd_ready = sem("var_ready"), sem("rstd_ready")
        xn_ready = sem("xn_ready")
        xb_ready = sem("xb_ready")
        xt_done, xt_copied = sem("xt_done"), sem("xt_copied")
        q_done = sem("q_done")
        q_copied, q_hi, q_full = sem("q_copied"), sem("q_hi"), sem("q_full")
        q_ready = sem("q_ready")
        s_done = sem("s_done")
        s_maxed, s_ready = sem("s_maxed"), sem("s_ready")
        p_ready = sem("p_ready")
        pt_done, pt_copied = sem("pt_done"), sem("pt_copied")
        pv_done = sem("pv_done")
        sum_rec, a_ready = sem("sum_rec"), sem("a_ready")
        at_done = sem("at_done")
        a_hi, a_lo = sem("a_hi"), sem("a_lo")
        o_done, x2_ready = sem("o_done"), sem("x2_ready")
        bn2_done, stats2_ready = sem("bn2_done"), sem("stats2_ready")
        var2_ready, rstd2_ready = sem("var2_ready"), sem("rstd2_ready")
        xf_ready, xft_done = sem("xf_ready"), sem("xft_done")
        xf_copied, xf_hi, xf_lo = sem("xf_copied"), sem("xf_hi"), sem("xf_lo")
        z_done = sem("z_done")
        route = sem("route")
        e_ready = sem("e_ready")
        c_moved = sem("c_moved")
        c3_hi, c3_lo = sem("c3_hi"), sem("c3_lo")
        c3t_done, c3t_copied = sem("c3t_done"), sem("c3t_copied")
        y_done, y_added = sem("y_done"), sem("y_added")
        pair_done = sem("pair_done")
        acc = sem("acc")
        h_ready, ht_done = sem("h_ready"), sem("ht_done")
        h_hi, h_lo = sem("h_hi"), sem("h_lo")
        stored = sem("stored")

        x_dram = x.rearrange("b (p j) d -> b p j d", j=TPB)
        out_dram = out.rearrange("b (p j) d -> p b j d", j=TPB)
        mask_dram = mask.rearrange("b (p j) k -> b p j k", j=TPB)
        rows = lambda w: w.rearrange("(c p) n -> p c n", c=C)
        w_dram = [w.rearrange("(c p) e o -> p c (e o)", c=C) for w in (w1_t, w2_t)]

        block = ctx.enter_context(nc.Block())

        @block.sync
        def _(sp):
            sp.dma_start(x_all[:, 0:1, :], x_dram[0][:, 0:1, :]).then_inc(x_in[0], 16)
            sp.dma_start(wk_sb[:, :, :], rows(wk_t)).then_inc(k_in, 16)
            sp.dma_start(wq_sb[:, :, :], rows(wq_t)).then_inc(q_in, 16)
            sp.dma_start(x_all[:, 1:2, :], x_dram[0][:, 1:2, :]).then_inc(x_in[1], 16)
            sp.dma_start(mask_all[:, 0:TPB, :], mask_dram[0]).then_inc(mask_in[0], 16)
            sp.dma_start(wv_sb[:, :, :], rows(wv_t)).then_inc(v_in, 16)
            sp.dma_start(bv_sb[:, :], bv.partition_broadcast(P)).then_inc(bv_in, 16)
            sp.dma_start(bo_sb[:, :], bo.partition_broadcast(P)).then_inc(bo_in, 16)
            sp.dma_start(x_all[:, 2:TPB, :], x_dram[0][:, 2:TPB, :]).then_inc(x_in[2], 16)
            sp.dma_start(wo_sb[:, :, :], rows(wo_t)).then_inc(o_in, 16)
            sp.dma_start(pw_sb[:, :], p_w).then_inc(ffn_in, 16)
            sp.dma_start(u_sb[:, :], u_t).then_inc(ffn_in, 16)
            for i in range(3):
                sp.dma_start(b2_sb[i * ROW:i * ROW + EXPERTS, :], b2).then_inc(ffn_in, 16)
            sp.dma_start(mask_all[:, TPB:T, :], mask_dram[1]).then_inc(mask_in[1], 16)
            sp.dma_start(x_all[:, TPB:T, :], x_dram[1]).then_inc(x_in[3], 16)
            for n in range(CHUNKS):
                layer, pair = n // PAIRS, n % PAIRS
                if n >= RING:
                    sp.wait_ge(w_split, n - RING + 1)
                sp.dma_start(stage[:, n % RING, :, :],
                             w_dram[layer][:, :, pair * 2 * D:(pair + 1) * 2 * D]).then_inc(w_in[n % RING], 16)

            def store(b, j, sums):
                sp.wait_ge(acc, sums)
                sp.dma_start(out_dram[:, b, j, :], x_all[:, j + b * TPB, :]).then_inc(stored, 16)

            for b in range(BATCH):
                with sp.Fori(0, TPB if b < BATCH - 1 else TPB - 1) as j:
                    store(b, j, 2 * SUMS * j + (2 * SUMS * b * TPB + 3 * SUMS))
            store(BATCH - 1, TPB - 1, 2 * SUMS * T)
            sp.wait_ge(stored, 16 * T)

        @block.gpsimd
        def _(pool):
            pool.memset(ident[:, :], 0.0).then_inc(consts_set, 1)
            pool.memset(ones[:, :], 1.0).then_inc(consts_set, 1)
            pool.memset(head_of[:, :], 1.0).then_inc(consts_set, 1)
            pool.memset(minus_half[:, :], -0.5).then_inc(consts_set, 1)
            pool.memset(eps[:, :], LN_EPS).then_inc(consts_set, 1)
            pool.memset(euler[:, :], EULER).then_inc(consts_set, 1)
            pool.iota(iota_e[:, :], pattern=[[1, EXPERTS]], base=0, channel_multiplier=0,
                      allow_small_or_imprecise_dtypes=True).then_inc(consts_set, 1)
            pool.wait_ge(consts_set, 7)
            pool.affine_select(out=ident[:, :], in_=ident[:, :], compare_op=ALU.not_equal, fill=1.0, base=0,
                               pattern=[[-1, P]], channel_multiplier=1).then_inc(consts_set, 1)
            pool.affine_select(out=head_of[:, :], in_=head_of[:, :], compare_op=ALU.is_ge, fill=0.0, base=0,
                               pattern=[[-DK, HPC]], channel_multiplier=1).then_inc(consts_set, 1)
            pool.wait_ge(consts_set, 9)
            pool.affine_select(out=head_of[:, :], in_=head_of[:, :], compare_op=ALU.is_ge, fill=0.0, base=DK - 1,
                               pattern=[[DK, HPC]], channel_multiplier=-1).then_inc(consts_set, 1)
            pool.wait_ge(consts_set, 10)
            pool.tensor_tensor(head_in[:, :], head_of[:, 0:HPG], head_of[:, HPG:HPC], ALU.add).then_inc(consts_set, 1)
            pool.memset(b2_hhl[:, :].bitcast(F32), 0.0).then_inc(consts_set, 1)
            pool.memset(c3_hlh[:, :, :], 0.0).then_inc(consts_set, 1)
            pool.memset(v_ext[:, :, :, :], 0.0).then_inc(consts_set, 1)
            pool.wait_ge(consts_set, 14)
            for side in range(2):
                pool.memset(v_ext[side * KEYS:(side + 1) * KEYS, :, :, side * VW + DK], 1.0).then_inc(consts_set, 1)
            pool.wait_ge(consts_set, 16)

            def inverse_deviation(t, stats, var, out_sem):
                pool.wait_ge(stats, t + 1)
                pool.tensor_tensor(var_eps[:, :], mean_var[:, 1:2], eps[:, :], ALU.add).then_inc(var, 1)
                pool.wait_ge(var, t + 1)
                pool.tensor_tensor(rstd[:, :], var_eps[:, :], minus_half[:, :], ALU.pow).then_inc(out_sem, 1)

            def add_output_bias(t):
                pool.wait_ge(xn_ready, t + 1)
                pool.tensor_tensor(x_all[:, t, :], x_all[:, t, :], bo_sb[:, :], ALU.add).then_inc(xb_ready, 1)

            def split_weights(n, slot):
                pool.wait_ge(w_hi, n + 1)
                pool.tensor_tensor(w_l[:, n, :, :], stage[:, slot, :, :], w_h[:, n, :, :].bitcast(F32),
                                   ALU.subtract).then_inc(w_split, 1)

            def attention(t):
                inverse_deviation(t, stats_ready, var_ready, rstd_ready)
                add_output_bias(t - 1)

            inverse_deviation(0, stats_ready, var_ready, rstd_ready)
            inverse_deviation(1, stats_ready, var_ready, rstd_ready)
            pool.wait_ge(setup_dve, 5)
            place_low_keys(pool, 0, kbd_set)
            inverse_deviation(2, stats_ready, var_ready, rstd_ready)
            pool.wait_ge(bo_in, 16)
            add_output_bias(0)
            add_output_bias(1)
            place_low_keys(pool, 1, kbd_set)
            attention(3)
            pool.wait_ge(kt_hh_set, 4)
            place_high_keys(pool, 1, kbd_set)
            pool.wait_ge(wo_hi, 1)
            pool.tensor_tensor(wo_l[:, :, :], wo_sb[:, :, :], wo_h[:, :, :].bitcast(F32),
                               ALU.subtract).then_inc(wo_lo, 1)
            attention(4)
            mask_keys(pool, 1, mask_set)
            with pool.Fori(0, CHUNKS // RING - 1) as g:
                for r in range(RING):
                    attention(g * RING + (r + 5))
                    split_weights(g * RING + r, r)
            for n in range(CHUNKS - RING, CHUNKS):
                if n < CHUNKS - 1:
                    attention(n + 5)
                else:
                    add_output_bias(T - 1)
                    inverse_deviation(0, stats2_ready, var2_ready, rstd2_ready)
                split_weights(n, n % RING)

            def exponentials(t):
                pool.wait_ge(route, ROUTE_STEPS * t + ROUTE_EXP)
                pool.tensor_tensor(top_e[:, :], euler[:, :], top_d[:, :, :].rearrange("p r k -> p (r k)"),
                                   ALU.pow).then_inc(e_ready, 1)

            def split_c3(t):
                if is_last(t):
                    pool.wait_ge(route, ROUTE_STEPS * T)
                else:
                    pool.wait_ge(c_moved, t + 1)
                if later(t, 1):
                    pool.wait_ge(c3t_done, t)
                pool.tensor_tensor(c3_hlh[:, 0:3:2, 0:EXPERTS].bitcast(F32R),
                                   weights2(t)[:, 2:3, :].to_broadcast([P, 2, EXPERTS]),
                                   ones[:, 0:2 * EXPERTS].rearrange("p (k e) -> p k e", k=2),
                                   ALU.mult).then_inc(c3_hi, 1)
                pool.wait_ge(c3_hi, t + 1)
                pool.tensor_tensor(c3_hlh[:, 1, 0:EXPERTS], weights2(t)[:, 2, :], c3_hlh[:, 0, 0:EXPERTS],
                                   ALU.subtract).then_inc(c3_lo, 1)

            exponentials(0)
            inverse_deviation(1, stats2_ready, var2_ready, rstd2_ready)
            exponentials(1)
            split_c3(0)
            with pool.Fori(2, T) as t:
                inverse_deviation(t, stats2_ready, var2_ready, rstd2_ready)
                exponentials(t)
                split_c3(t - 1)
            split_c3(T - 1)

        @block.scalar
        def _(act):
            act.dma_start(ctx_sb[:, :, :], rows(ctx_t)).then_inc(ctx_in, 16)
            act.dma_start(bk_sb[:, :], bk).then_inc(ctx_in, 16)
            act.dma_start(bq_sb[:, :], bq).then_inc(bq_in, 16)

            def copy_xt(t):
                act.wait_ge(xt_done, t + 1)
                if later(t, 1):
                    act.wait_ge(q_done, t)
                nc.scalar.activation(xn_t[:, :, :], ps_x, ACT.Copy).then_inc(xt_copied, 1)

            def q_high(t):
                act.wait_ge(q_done, t + 1)
                if later(t, 1):
                    act.wait_ge(q_ready, t)
                    act.wait_ge(q_full, t)
                for c in range(C):
                    nc.scalar.activation(q[:, c, :], ps_q[:, c, :], ACT.Identity,
                                         bias=bq_sb[:, c:c + 1]).then_inc(q_copied, 1)
                act.wait_ge(q_copied, C * t + C)
                if later(t, 1):
                    act.wait_ge(s_done, t)
                for group in range(2):
                    r = slice(group * HALF, (group + 1) * HALF)
                    nc.scalar.activation(q_hl[r, :, group, :], q[r, :, :], ACT.Copy).then_inc(q_hi, 1)
                nc.scalar.activation(q_h[:, :, :], q[:, :, :], ACT.Copy).then_inc(q_full, 1)

            def exp_scores(t):
                act.wait_ge(s_ready, t + 1)
                if later(t, 1):
                    act.wait_ge(pt_done, 2 * t)
                nc.scalar.activation(prob[:, :, :], s_d[:, :, :], ACT.Exp).then_inc(p_ready, 1)

            def copy_pt(t):
                if later(t, 1):
                    act.wait_ge(pv_done, t)
                for half in range(2):
                    act.wait_ge(pt_done, 2 * t + half + 1)
                    j = half * HP // 2
                    nc.scalar.activation(prob_t[:, j:j + HP // 2, :], ps_pt[:, j:j + HP // 2, :],
                                         ACT.Copy).then_inc(pt_copied, 1)

            def a_high(t):
                act.wait_ge(at_done, t + 1)
                if later(t, 1):
                    act.wait_ge(o_done, t)
                nc.scalar.activation(a_h[:, :, :], ps_a, ACT.Copy).then_inc(a_hi, 1)

            def copy_xf(t):
                act.wait_ge(xft_done, t + 1)
                if later(t, 1):
                    act.wait_ge(z_done, t)
                    act.wait_ge(xf_lo, t)
                nc.scalar.activation(xf_t[:, :, :], ps_t, ACT.Copy).then_inc(xf_copied, 1)
                act.wait_ge(xf_copied, t + 1)
                nc.scalar.activation(xf_h[:, :, :], xf_t[:, :, :], ACT.Copy).then_inc(xf_hi, 1)

            act.wait_ge(consts_set, 8)
            nc.scalar.activation(ident_b[:, :], ident[:, :], ACT.Copy).then_inc(ident_b_set, 1)
            copy_xt(0)
            act.wait_ge(setup_dve, 3)
            for group in range(2):
                for half in range(2):
                    nc.scalar.activation(kt_hh[half * HALF:(half + 1) * HALF, :, group, :].bitcast(F32R),
                                         kt[group * HALF:(group + 1) * HALF, :, :], ACT.Copy).then_inc(kt_hh_set, 1)
            act.wait_ge(bq_in, 16)
            q_high(0)
            copy_xt(1)
            q_high(1)
            exp_scores(0)
            copy_xt(2)
            act.wait_ge(o_in, 16)
            nc.scalar.activation(wo_h[:, :, :], wo_sb[:, :, :], ACT.Copy).then_inc(wo_hi, 1)
            act.wait_ge(ffn_in, 80)
            act.wait_ge(consts_set, 12)
            for i in range(3):
                r = slice(i * ROW, i * ROW + EXPERTS)
                nc.scalar.activation(b2_hhl[r, :], b2_sb[r, :], ACT.Copy).then_inc(b2_hi, 1)

            copy_pt(0)
            q_high(2)
            exp_scores(1)
            copy_xt(3)

            def attention(t):
                copy_pt(t)
                a_high(t - 1)
                q_high(t + 2)
                exp_scores(t + 1)

            def split_weights(g, r):
                act.wait_ge(w_in[r], g * 16 + 16)
                nc.scalar.activation(w_h[:, g * RING + r, :, :], stage[:, r, :, :], ACT.Copy).then_inc(w_hi, 1)

            attention(1)
            copy_xt(4)
            with act.Fori(0, CHUNKS // RING - 1) as g:
                for r in range(RING):
                    attention(g * RING + (r + 2))
                    split_weights(g, r)
                    copy_xt(g * RING + (r + 5))
            for r in range(RING):
                attention(T - 2 - RING + r)
                split_weights(CHUNKS // RING - 1, r)
                if r < RING - 1:
                    copy_xt(T + 1 - RING + r)
            copy_xf(0)
            copy_pt(T - 2)
            a_high(T - 3)
            exp_scores(T - 1)
            copy_pt(T - 1)
            a_high(T - 2)
            a_high(T - 1)
            copy_xf(1)

            def h_high(t):
                act.wait_ge(ht_done, t + 1)
                nc.scalar.activation(h_buffers(t)[0][:, :, :], ps_t, ACT.Copy).then_inc(h_hi, 1)

            def copy_c3t(t):
                act.wait_ge(c3t_done, t + 1)
                nc.scalar.activation(c3_t[:, :], ps_c3, ACT.Copy).then_inc(c3t_copied, 1)

            def gelu(t, acc_count):
                act.wait_ge(acc, acc_count)
                if later(t, 1):
                    act.wait_ge(ht_done, t)
                nc.scalar.activation(h[:, :], h_in[:, :], ACT.Gelu).then_inc(h_ready, 1)

            gelu(0, SUMS)

            def experts(t):
                h_high(t)
                copy_c3t(t)
                gelu(t + 1, SUMS * 2 * (t + 1))
                copy_xf(t + 2)

            experts(0)
            with act.Fori(1, T - 2) as t:
                experts(t)
            h_high(T - 2)
            copy_c3t(T - 2)
            gelu(T - 1, SUMS * 2 * (T - 1))
            h_high(T - 1)
            copy_c3t(T - 1)

        @block.vector
        def _(dve):
            def statistics(t, src, done, ready):
                dve.bn_stats(bn[:, :], src[:, t, :]).then_inc(done, 1)
                dve.wait_ge(done, t + 1)
                dve.memset(waited[:, :], 0.0)
                dve.bn_aggr(mean_var[:, :], bn[:, :]).then_inc(ready, 1)

            def normalise(t, src, dst, rstd_sem, ready):
                dve.wait_ge(rstd_sem, t + 1)
                dve.tensor_scalar(dst[:, :], src[:, t, :], mean_var[:, 0:1], rstd[:, 0:1],
                                  ALU.subtract, ALU.mult).then_inc(ready, 1)

            def stats1(t):
                statistics(t, x_all, bn_done, stats_ready)

            def normalise1(t):
                if later(t, 1):
                    dve.wait_ge(xt_done, t)
                normalise(t, x_all, xn, rstd_ready, xn_ready)

            def normalise2(t):
                dve.wait_ge(xft_done, t)
                normalise(t, x_all, xf, rstd2_ready, xf_ready)

            def q_low(t):
                dve.wait_ge(q_hi, 2 * t + 2)
                if later(t, 1):
                    dve.wait_ge(s_done, t)
                for group in range(2):
                    r = slice(group * HALF, (group + 1) * HALF)
                    other = slice((1 - group) * HALF, (2 - group) * HALF)
                    ins = dve.tensor_tensor(q_hl[other, :, group, :], q[r, :, :], q_hl[r, :, group, :].bitcast(F32),
                                            ALU.subtract)
                ins.then_inc(q_ready, 1)

            def max_scores(t):
                dve.wait_ge(s_done, t + 1)
                dve.tensor_reduce(s_max[:, :], ps_s, AX_X, ALU.max).then_inc(s_maxed, 1)

            def subtract_max(t):
                if later(t, 1):
                    dve.wait_ge(p_ready, t)
                dve.wait_ge(s_maxed, t + 1)
                dve.tensor_tensor(s_d[:, :, :], ps_s, s_max[:, :].unsqueeze(2).to_broadcast([P, HEADS, KEYS]),
                                  ALU.subtract).then_inc(s_ready, 1)

            def divide_by_sum(t):
                dve.wait_ge(pv_done, t + 1)
                pv = ps_v.rearrange("p (h v) -> p h v", v=VW)
                dve.reciprocal(r_sum[:, :], pv[:, :, DK]).then_inc(sum_rec, 1)
                dve.wait_ge(sum_rec, t + 1)
                if later(t, 1):
                    dve.wait_ge(at_done, t)
                dve.tensor_tensor(a_n[:, :].rearrange("p (h v) -> p h v", v=DK), pv[:, :, 0:DK],
                                  r_sum[:, :].unsqueeze(2).to_broadcast([P, HEADS, DK]),
                                  ALU.mult).then_inc(a_ready, 1)

            def a_low(t):
                dve.wait_ge(a_hi, t + 1)
                if later(t, 1):
                    dve.wait_ge(o_done, t)
                dve.tensor_tensor(a_l[:, :, :], ps_a, a_h[:, :, :].bitcast(F32), ALU.subtract).then_inc(a_lo, 1)

            def add_attention(t):
                dve.wait_ge(o_done, t + 1)
                dve.wait_ge(xb_ready, t + 1)
                o = ps_o_last if is_last(t) else ps_o
                dve.tensor_tensor(x_all[:, t, :], o, x_all[:, t, :], ALU.add).then_inc(x2_ready, 1)

            dve.wait_ge(x_in[0], 16)
            stats1(0)
            normalise1(0)
            dve.wait_ge(ctx_in, 32)
            dve.tensor_copy(ctx_dup[:, :, :, :, :],
                            ctx_sb[:, :, :].rearrange("p c (b k) -> p (c b) k", b=BATCH).unsqueeze(2)
                            .to_broadcast([P, C * BATCH, 2, KEYS])).then_inc(setup_dve, 1)
            dve.wait_ge(x_in[1], 16)
            stats1(1)
            dve.wait_ge(kt_done, C)
            for c in range(C):
                dve.tensor_scalar(kt[:, c, :], banks[:, 0, c * P:(c + 1) * P], bk_sb[:, c:c + 1], SCALE,
                                  ALU.add, ALU.mult).then_inc(setup_dve, 1)
            dve.wait_ge(setup_dve, 3)
            dve.tensor_copy(kt_h[:, :, :].bitcast(F32R), kt[:, :, :]).then_inc(setup_dve, 1)
            dve.wait_ge(setup_dve, 4)
            dve.tensor_tensor(kt_l[:, :, :], kt[:, :, :], kt_h[:, :, :], ALU.subtract).then_inc(setup_dve, 1)
            normalise1(1)
            dve.wait_ge(consts_set, 11)
            dve.wait_ge(kt_hh_set, 4)
            place_high_keys(dve, 0, setup_dve)
            mask_keys(dve, 0, setup_dve)
            q_low(0)
            dve.wait_ge(x_in[2], 16)
            stats1(2)
            def add_value_bias(b):
                dve.wait_ge(v_done, b + 1)
                for side in range(2):
                    r = slice(side * KEYS, (side + 1) * KEYS)
                    v = banks[r, 2 + b, 0:D].rearrange("p (j s v) -> p j s v", s=2, v=DK)[:, :, side, :]
                    bias = bv_sb[r, :].rearrange("p (j s v) -> p j s v", s=2, v=DK)[:, :, side, :]
                    dve.tensor_tensor(v_ext[r, b, :, side * VW:side * VW + DK], v, bias,
                                      ALU.add).then_inc(setup_dve, 1)

            dve.wait_ge(consts_set, 16)
            dve.wait_ge(bv_in, 16)
            add_value_bias(0)

            max_scores(0)
            normalise1(2)
            subtract_max(0)
            q_low(1)
            stats1(3)
            add_value_bias(1)

            max_scores(1)
            subtract_max(1)
            normalise1(3)
            q_low(2)
            dve.wait_ge(g_done, 1)
            dve.tensor_copy(router_w[:, :, :], ps_g).then_inc(setup_dve, 1)
            divide_by_sum(0)
            stats1(4)
            dve.wait_ge(b2_hi, 3)
            r = slice(2 * ROW, 2 * ROW + EXPERTS)
            dve.tensor_tensor(b2_hhl[r, :], b2_sb[r, :], b2_hhl[r, :].bitcast(F32),
                              ALU.subtract).then_inc(setup_dve, 1)

            def attention(t):
                max_scores(t + 1)
                subtract_max(t + 1)
                a_low(t - 1)
                normalise1(t + 3)
                q_low(t + 2)
                divide_by_sum(t)
                add_attention(t - 1)

            attention(1)
            stats1(5)
            dve.wait_ge(x_in[3], 16)
            with dve.Fori(2, T - 4) as t:
                attention(t)
                stats1(t + 4)
            attention(T - 4)
            statistics(0, x_all, bn2_done, stats2_ready)

            def xf_low(t):
                dve.wait_ge(xf_hi, t + 1)
                dve.tensor_tensor(xf_l[:, :, :], xf_t[:, :, :], xf_h[:, :, :].bitcast(F32), ALU.subtract).then_inc(xf_lo, 1)

            def h_low(t):
                dve.wait_ge(h_hi, t + 1)
                high, low = h_buffers(t)
                dve.tensor_tensor(low[:, :, :], ps_t, high[:, :, :].bitcast(F32), ALU.subtract).then_inc(h_lo, 1)

            def find_top(t):
                n = ROUTE_STEPS * t
                dve.wait_ge(z_done, t + 1)
                dve.tensor_copy(z_sb[:, :, :].rearrange("p r e -> p (r e)"), ps_z).then_inc(route, 1)
                dve.wait_ge(route, n + ROUTE_Z)
                dve.memset(waited[:, :], 0.0)
                for r in range(3):
                    dve.max(top[:, r, :], z_sb[:, r, :]).then_inc(route, 1)
                dve.wait_ge(route, n + ROUTE_TOP)
                if later(t, 1):
                    dve.wait_ge(e_ready, t)
                dve.tensor_tensor(top_d[:, :, :], top[:, :, 0:TOP_K],
                                  top[:, :, 0:1].to_broadcast([P, 3, TOP_K]), ALU.subtract).then_inc(route, 1)
                for r in range(3):
                    dve.max_index(top_i[:, r, :], top[:, r, :], z_sb[:, r, :]).then_inc(route, 1)

            def combine_weights(t):
                n = ROUTE_STEPS * t + ROUTE_INDEX
                dve.wait_ge(route, n)
                dve.tensor_tensor(at_e[:, :, :, :],
                                  top_i[:, :, 0:TOP_K].unsqueeze(2).to_broadcast([P, 3, EXPERTS, TOP_K]),
                                  iota_e[:, :].unsqueeze(1).unsqueeze(3).to_broadcast([P, 3, EXPERTS, TOP_K]),
                                  ALU.is_equal).then_inc(route, 1)
                dve.wait_ge(e_ready, t + 1)
                e = top_e[:, :].rearrange("p (r k) -> p r k", r=3)
                dve.tensor_reduce(e_sum[:, :], e, AX_X, ALU.add).then_inc(route, 1)
                dve.wait_ge(route, n + 2)
                dve.reciprocal(e_rec[:, :], e_sum[:, :]).then_inc(route, 1)
                dve.wait_ge(route, n + 3)
                dve.tensor_tensor(top_w[:, :, :], e, e_rec[:, :].unsqueeze(2).to_broadcast([P, 3, TOP_K]),
                                  ALU.mult).then_inc(route, 1)
                dve.wait_ge(route, n + 4)
                dve.tensor_tensor(w_at_e[:, :, :, :], at_e[:, :, :, :],
                                  top_w[:, :, :].unsqueeze(2).to_broadcast([P, 3, EXPERTS, TOP_K]),
                                  ALU.mult).then_inc(route, 1)
                dve.wait_ge(route, n + 5)
                if later(t, 1):
                    dve.wait_ge(c_moved, t)
                dve.tensor_reduce(c_new[:, :, :], w_at_e[:, :, :, :], AX_X, ALU.add).then_inc(route, 1)

            def move_weights(t):
                dve.wait_ge(route, ROUTE_STEPS * (t + 1))
                if later(t, 1):
                    dve.wait_ge(c3t_done, t)
                    dve.wait_ge(acc, SUMS * (2 * t + 1))
                dve.tensor_copy(c_cur[:, :, :], c_new[:, :, :]).then_inc(c_moved, 1)

            def sum_pair(slot, pair, weights, sums, added):
                dve.wait_ge(pair_done, PAIRS * slot + pair + 1)
                for e in (2 * pair, 2 * pair + 1):
                    product = banks[:, BANK[pair], (e % 2) * D:(e % 2 + 1) * D]
                    if pair == 0 and e >= added:
                        dve.tensor_scalar(sums[e % 2][:, :], product, weights[:, e:e + 1], None,
                                          ALU.mult).then_inc(acc, 1)
                        continue
                    if pair > 0:
                        dve.wait_ge(acc, SUMS * slot + e - 1)
                    dve.scalar_tensor_tensor(out=sums[e % 2][:, :], in0=product, scalar=weights[:, e:e + 1],
                                             in1=sums[e % 2][:, :], op0=ALU.mult, op1=ALU.add).then_inc(acc, 1)

            def last_sum(slot, sums, dst):
                dve.wait_ge(acc, SUMS * slot + EXPERTS)
                dve.tensor_tensor(dst, sums[0][:, :], sums[1][:, :], ALU.add).then_inc(acc, 1)

            def layer1_pairs(t, pairs, last=True):
                for pair in pairs:
                    if pair == 0:
                        dve.wait_ge(route, ROUTE_STEPS * (t + 1))
                    if pair == 0 and later(t, 1):
                        dve.wait_ge(h_ready, t)
                    sum_pair(slot1(t), pair, c_new[:, 0, :], sum1, 0)
                    if pair == PAIRS - 1 and last:
                        last_sum(slot1(t), sum1, h_in[:, :])

            def start_layer2(t):
                dve.wait_ge(y_done, t + 1)
                if is_last(t):
                    dve.wait_ge(acc, SUMS * slot2(t))
                dve.tensor_tensor(sum2[0][:, :], ps_y, x_all[:, t, :], ALU.add).then_inc(y_added, 1)
                dve.wait_ge(y_added, t + 1)
                if not is_last(t):
                    dve.wait_ge(c_moved, t + 1)

            def layer2_pairs(t, pairs):
                for pair in pairs:
                    sum_pair(slot2(t), pair, weights2(t)[:, 1, :], sum2, 1)
                    if pair == PAIRS - 1:
                        last_sum(slot2(t), sum2, x_all[:, t, :])

            max_scores(T - 2)
            subtract_max(T - 2)
            a_low(T - 4)
            normalise(0, x_all, xf, rstd2_ready, xf_ready)
            q_low(T - 1)
            divide_by_sum(T - 3)
            add_attention(T - 4)
            statistics(1, x_all, bn2_done, stats2_ready)
            xf_low(0)

            max_scores(T - 1)
            subtract_max(T - 1)
            a_low(T - 3)
            find_top(0)
            divide_by_sum(T - 2)
            add_attention(T - 3)
            combine_weights(0)
            normalise2(1)

            layer1_pairs(0, range(0, 2))
            a_low(T - 2)
            divide_by_sum(T - 1)
            add_attention(T - 2)
            layer1_pairs(0, range(2, 3))
            a_low(T - 1)
            layer1_pairs(0, range(3, PAIRS), last=False)
            add_attention(T - 1)
            xf_low(1)
            last_sum(0, sum1, h_in[:, :])
            find_top(1)
            move_weights(0)
            combine_weights(1)

            def experts(t, ahead=True):
                if ahead:
                    statistics(t + 2, x_all, bn2_done, stats2_ready)
                layer1_pairs(t + 1, range(0, 3))
                h_low(t)
                if ahead:
                    normalise2(t + 2)
                layer1_pairs(t + 1, range(3, PAIRS))
                start_layer2(t)
                layer2_pairs(t, range(0, 1))
                if ahead:
                    xf_low(t + 2)
                layer2_pairs(t, range(1, 4))
                if ahead:
                    find_top(t + 2)
                else:
                    h_low(t + 1)
                layer2_pairs(t, range(4, PAIRS))
                if ahead:
                    move_weights(t + 1)
                    combine_weights(t + 2)

            experts(0)
            with dve.Fori(1, T - 2) as t:
                experts(t)
            experts(T - 2, ahead=False)
            start_layer2(T - 1)
            layer2_pairs(T - 1, range(PAIRS))

        @block.tensor
        def _(pe):
            def split_product(dst, left, right):
                (lh, ll), (rh, rl) = left, right
                terms = [(c, a, b) for c in range(C) for a, b in ((lh, rh), (ll, rh), (lh, rl))]
                for i, (c, a, b) in enumerate(terms):
                    ins = pe.matmul(dst, a(c), b(c), start=(i == 0), stop=(i == len(terms) - 1))
                return ins

            def whole(w):
                return lambda c: w[:, c, :]

            def keys_project(m):
                for c in range(C):
                    ins = pe.matmul(banks[:, 0, m * P:(m + 1) * P], wk_sb[:, c, m * P:(m + 1) * P],
                                    ctx_sb[:, c, :], start=(c == 0), stop=(c == C - 1))
                ins.then_inc(kt_done, 1)

            def values_project(b):
                pe.wait_ge(v_in, 16)
                pe.wait_ge(setup_dve, 1)
                for c in range(C):
                    ins = pe.matmul(banks[:, 2 + b, 0:D], ctx_dup[:, c, b, :, :].rearrange("p s k -> p (s k)"),
                                    wv_sb[:, c, :], start=(c == 0), stop=(c == C - 1))
                ins.then_inc(v_done, 1)

            def router_weights():
                pe.wait_ge(ffn_in, 80)
                for c in range(C):
                    ins = pe.matmul(ps_g[:, c, :], pw_sb[:, c * P:(c + 1) * P],
                                    u_sb[:, :], start=True, stop=True)
                ins.then_inc(g_done, 1)

            def transpose_x(t):
                pe.wait_ge(xn_ready, t + 1)
                if later(t, 1):
                    pe.wait_ge(xt_copied, t)
                for c in range(C):
                    ins = pe.transpose(ps_x[:, c, :], xn[:, c * P:(c + 1) * P], ident[:, :])
                ins.then_inc(xt_done, 1)

            def queries(t):
                pe.wait_ge(xt_copied, t + 1)
                if later(t, 1):
                    pe.wait_ge(q_copied, C * t)
                for m in range(C):
                    for c in range(C):
                        ins = pe.matmul(ps_q[:, m, :], wq_sb[:, c, m * P:(m + 1) * P], xn_t[:, c, :],
                                        start=(c == 0), stop=(c == C - 1))
                ins.then_inc(q_done, 1)

            def scores(t, b):
                pe.wait_ge(q_ready, t + 1)
                pe.wait_ge(q_full, t + 1)
                if later(t, 1):
                    pe.wait_ge(s_ready, t)
                for c in range(C):
                    pe.matmul(banks[:, c, :].rearrange("p (h k) -> p h k", k=KEYS), ident_b[:, :],
                              mask_bias[:, t, :].unsqueeze(1).to_broadcast([P, HPC, KEYS]), start=True, stop=False)
                    for group in range(2):
                        pe.matmul(banks[:, c, group * HPG * KEYS:(group + 1) * HPG * KEYS], q_hl[:, c, group, :],
                                  kbd_hh[:, b, c, group, :, :].rearrange("p h k -> p (h k)"), start=False, stop=False)
                    ins = pe.matmul(banks[:, c, :], q_h[:, c, :], kbd_l[:, b, c, :, :].rearrange("p h k -> p (h k)"),
                                    start=False, stop=True)
                ins.then_inc(s_done, 1)

            def transpose_probs(t):
                pe.wait_ge(p_ready, t + 1)
                if later(t, 1):
                    pe.wait_ge(pt_copied, 2 * t)
                for half in range(2):
                    for j in range(half * HP // 2, (half + 1) * HP // 2):
                        ins = pe.transpose(ps_pt[:, j, :], prob[:, 2 * j:2 * j + 2, :].rearrange("p h k -> p (h k)"),
                                           ident[:, :])
                    ins.then_inc(pt_done, 1)

            def weigh_values(t, b):
                if later(t, 1):
                    pe.wait_ge(a_ready, t)
                for half in range(2):
                    pe.wait_ge(pt_copied, 2 * t + half + 1)
                    for j in range(half * HP // 2, (half + 1) * HP // 2):
                        ins = pe.matmul(ps_v[:, j * 2 * VW:(j + 1) * 2 * VW], prob_t[:, j, :], v_ext[:, b, j, :],
                                        start=True, stop=True)
                ins.then_inc(pv_done, 1)

            def transpose_a(t):
                pe.wait_ge(a_ready, t + 1)
                if later(t, 1):
                    pe.wait_ge(x2_ready, t)
                else:
                    pe.wait_ge(setup_dve, V_SET + 1)
                for c in range(C):
                    ins = pe.transpose(ps_a[:, c, :], a_n[:, c * P:(c + 1) * P], ident[:, :])
                ins.then_inc(at_done, 1)

            def output_project(t):
                if isinstance(t, int) and t == 0:
                    pe.wait_ge(wo_lo, 1)
                pe.wait_ge(a_lo, t + 1)
                o = ps_o_last if is_last(t) else ps_o
                split_product(o, (whole(a_h), whole(a_l)), (whole(wo_h), whole(wo_l))).then_inc(o_done, 1)

            def transpose_xf(t):
                pe.wait_ge(xf_ready, t + 1)
                if later(t, 2):
                    pe.wait_ge(h_lo, t - 1)
                else:
                    pe.wait_ge(xf_copied if t else xt_copied, 1 if t else T)
                for c in range(C):
                    ins = pe.transpose(ps_t[:, c, :], xf[:, c * P:(c + 1) * P], ident[:, :])
                ins.then_inc(xft_done, 1)

            def logits(t):
                pe.wait_ge(xf_copied, t + 1)
                if later(t, 2):
                    pe.wait_ge(y_added, t - 1)
                elif t == 1:
                    pe.wait_ge(x2_ready, T)
                for c in range(C):
                    ins = pe.matmul(ps_z, xf_t[:, c, :], router_w[:, c, :], start=(c == 0), stop=(c == C - 1))
                ins.then_inc(z_done, 1)

            def transpose_h(t):
                pe.wait_ge(h_ready, t + 1)
                n = min(t + 2, T) if isinstance(t, int) else t + 2
                pe.wait_ge(xf_copied, n)
                for c in range(C):
                    ins = pe.transpose(ps_t[:, c, :], h[:, c * P:(c + 1) * P], ident[:, :])
                ins.then_inc(ht_done, 1)

            def transpose_c3(t):
                pe.wait_ge(c3_lo, t + 1)
                if later(t, 1):
                    pe.wait_ge(y_added, t)
                pe.transpose(ps_c3, c3_hlh[:, :, :].rearrange("p k r -> p (k r)"), ident[:, :]).then_inc(c3t_done, 1)

            def expert_bias(t):
                pe.wait_ge(c3t_copied, t + 1)
                pe.matmul(ps_y, c3_t[:, :], b2_hhl[:, :], start=True, stop=True).then_inc(y_done, 1)

            def expert_pairs(slot, pairs, left, layer):
                for pair in pairs:
                    if later(slot, 1):
                        pe.wait_ge(acc, SUMS * slot - SUMS + 2 * pair + 2)
                    n = layer * PAIRS + pair
                    split_product(banks[:, BANK[pair], :], left,
                                  (lambda c: w_h[:, n, c, :], lambda c: w_l[:, n, c, :])).then_inc(pair_done, 1)

            xf_parts, h_parts = (whole(xf_h), whole(xf_l)), (whole(h_h), whole(h_l))

            pe.wait_ge(k_in, 16)
            pe.wait_ge(ctx_in, 32)
            keys_project(0)
            pe.wait_ge(consts_set, 8)
            transpose_x(0)
            keys_project(1)
            pe.wait_ge(q_in, 16)
            queries(0)
            transpose_x(1)
            values_project(0)
            pe.wait_ge(setup_dve, KBD)
            pe.wait_ge(kbd_set, 1)
            pe.wait_ge(ident_b_set, 1)
            scores(0, 0)
            queries(1)
            values_project(1)
            router_weights()
            transpose_x(2)

            scores(1, 0)
            pe.wait_ge(setup_dve, V_SET)
            transpose_probs(0)
            queries(2)
            weigh_values(0, 0)
            transpose_x(3)

            def attention(t, b, b_next):
                scores(t + 1, b_next)
                transpose_probs(t)
                transpose_a(t - 1)
                queries(t + 2)
                weigh_values(t, b)
                output_project(t - 1)

            attention(1, 0, 0)
            transpose_x(4)
            pe.wait_ge(kbd_set, 3)
            pe.wait_ge(mask_set, 1)
            pe.wait_ge(setup_dve, SETUP)
            with pe.Fori(2, T - 3) as t:
                attention(t, t // TPB, (t + 1) // TPB)
                transpose_x(t + 3)

            attention(T - 3, BATCH - 1, BATCH - 1)
            transpose_xf(0)

            scores(T - 1, BATCH - 1)
            transpose_probs(T - 2)
            transpose_a(T - 3)
            logits(0)
            weigh_values(T - 2, BATCH - 1)
            output_project(T - 3)

            pe.wait_ge(w_split, PAIRS)
            pe.wait_ge(s_ready, T)
            pe.wait_ge(xf_lo, 1)
            expert_pairs(0, range(0, 2), xf_parts, 0)
            transpose_probs(T - 1)
            transpose_a(T - 2)
            weigh_values(T - 1, BATCH - 1)
            output_project(T - 2)
            expert_pairs(0, range(2, 4), xf_parts, 0)
            transpose_a(T - 1)
            expert_pairs(0, range(4, 5), xf_parts, 0)
            pe.wait_ge(a_lo, T)
            expert_pairs(0, range(5, PAIRS), xf_parts, 0)
            transpose_xf(1)
            output_project(T - 1)
            logits(1)
            pe.wait_ge(w_split, CHUNKS)

            def experts(t, ahead=True):
                pe.wait_ge(xf_lo, t + 2)
                expert_pairs(slot1(t + 1), range(0, 3), xf_parts, 0)
                transpose_h(t)
                transpose_c3(t)
                expert_pairs(slot1(t + 1), range(3, PAIRS), xf_parts, 0)
                expert_bias(t)
                pe.wait_ge(h_lo, t + 1)
                if ahead:
                    transpose_xf(t + 2)
                expert_pairs(slot2(t), range(0, 3), h_parts, 1)
                if ahead:
                    logits(t + 2)
                else:
                    transpose_h(t + 1)
                    transpose_c3(t + 1)
                expert_pairs(slot2(t), range(3, PAIRS), h_parts, 1)

            experts(0)
            with pe.Fori(1, T - 2) as t:
                experts(t)
            experts(T - 2, ahead=False)
            expert_bias(T - 1)
            pe.wait_ge(h_lo, T)
            expert_pairs(2 * T - 1, range(PAIRS), [whole(part) for part in h_buffers(T - 1)], 1)


_INS = ["x", "mask", "ctx_t", "wq_t", "bq", "wk_t", "bk", "wv_t", "bv", "wo_t", "bo", "p_w", "u_t", "w1_t", "w2_t", "b2"]
_OUTS = [((2, 1024, 256), "float32")]


def kernel(x, ctx_1024, mask_BxSxS2_ik1, L0_xattn_Wq, L0_xattn_bq, L0_xattn_Wk, L0_xattn_bk, L0_xattn_Wv,
           L0_xattn_bv, L0_xattn_Wo, L0_xattn_bo, L0_ffn_P_w, L0_ffn_U1, L0_ffn_U2, L0_ffn_U3, L0_ffn_W1,
           L0_ffn_W2, L0_ffn_b2):
    import numpy as _np
    import concourse.bacc as _bacc
    from concourse import mybir as _mybir
    from concourse.bass_utils import run_bass_kernel_spmd as _run

    d = x.shape[-1]
    columns = lambda v: _np.asarray(v).reshape(-1, P).T
    laid_out = {
        "x": x, "mask": mask_BxSxS2_ik1,
        "ctx_t": _np.asarray(ctx_1024).reshape(-1, d).T,
        "wq_t": _np.asarray(L0_xattn_Wq).T, "bq": columns(L0_xattn_bq),
        "wk_t": _np.asarray(L0_xattn_Wk).T, "bk": columns(L0_xattn_bk),
        "wv_t": _np.asarray(L0_xattn_Wv).T, "bv": _np.asarray(L0_xattn_bv),
        "wo_t": _np.asarray(L0_xattn_Wo).T, "bo": _np.asarray(L0_xattn_bo),
        "p_w": L0_ffn_P_w,
        "u_t": _np.concatenate([_np.asarray(u) for u in (L0_ffn_U1, L0_ffn_U2, L0_ffn_U3)], axis=0).T,
        "w1_t": _np.asarray(L0_ffn_W1).transpose(2, 0, 1), "w2_t": _np.asarray(L0_ffn_W2).transpose(2, 0, 1),
        "b2": L0_ffn_b2,
    }
    nc = _bacc.Bacc("TRN2", target_bir_lowering=False, num_devices=1)
    arrays, args = {}, []
    for name in _INS:
        a = _np.ascontiguousarray(laid_out[name])
        arrays[f"in_{name}_dram"] = a
        args.append(nc.dram_tensor(f"in_{name}_dram", a.shape, _mybir.dt.from_np(a.dtype), kind="ExternalInput").ap())
    for i, (shape, dtype) in enumerate(_OUTS):
        dt = _mybir.dt.from_np(_np.dtype(dtype))
        args.append(nc.dram_tensor(f"out_{i}_dram", shape, dt, kind="ExternalOutput").ap())
    xattn_ffn_kernel(nc, *args)
    r = _run(nc, [arrays], core_ids=[0])
    return r.results[0]["out_0_dram"]
```
